# Optimizing a Trainium2 kernel written in Bass

```python
import numpy as np
import jax
import jax.numpy as jnp

def _softmax(x, axis=-1):
    return jax.nn.softmax(x, axis=axis)

def _gelu(x):
    return jax.nn.gelu(x, approximate=True)

def _silu(x):
    return jax.nn.silu(x)

def _sigmoid(x):
    return jax.nn.sigmoid(x)

def _layernorm(x, axis=-1, eps=1e-05):
    m = jnp.mean(x, axis=axis, keepdims=True)
    v = jnp.var(x, axis=axis, keepdims=True)
    return (x - m) / jnp.sqrt(v + eps)

def _scatter_add(tgt, idx, src, axis=0):
    return tgt.at[idx].add(src)

def _segment_sum(src, seg, n):
    return jax.ops.segment_sum(src, seg, n)
kernel_name = 'mk_adj_preln_d2_adj_r2_1bc0d6'

def setup_inputs(seed: int=0):
    np.random.seed(seed)
    _w = jnp.asarray

    def _rec_inputs():
        import jax
        import jax.numpy as jnp
        _gk = jax.random.key(seed)
        x = -0.0005207 + 1.001 * jax.random.normal(jax.random.fold_in(_gk, 1), (8192, 128), jnp.float32)
        _w = (1.0 + jnp.arange(8192, dtype=jnp.float32)) ** (-0.5)
        _w = _w / _w.mean()
        _pij = jnp.clip(0.000244141 * _w[:, None] * _w[None, :], 0.0, 1.0)
        _a = jax.random.uniform(jax.random.fold_in(_gk, 2), (8192, 8192)) < _pij
        _a = jnp.logical_or(_a, jnp.swapaxes(_a, -1, -2))
        _a = jnp.logical_or(_a, jnp.eye(8192, dtype=bool))
        _af = _a.astype(jnp.float32)
        _af = _af * jax.random.uniform(jax.random.fold_in(_gk, 3), (8192, 8192), jnp.float32, 0.05, 2.05)
        adj = _af
        return (x, adj)
    x, adj = _rec_inputs()

    def _L0_gnn_setup():
        import jax, jax.numpy as jnp
        import numpy as np
        N = 4096
        D = 128
        CUTOFF = 1.0
        MU = 1.0
        SIGMA = 0.5

        def sensitivity(r, mu, sigma):
            return jnp.exp(-(1.0 / r - 1.0 / mu) ** 2 / (2.0 * sigma * sigma))
        key = jax.random.key(seed)
        k_z, k_d, k_w = jax.random.split(key, 3)
        z = jax.random.normal(k_z, (N, D), dtype=jnp.float32)
        dist_matrix = jax.random.uniform(k_d, (N, N), dtype=jnp.float32) * 2.0 + 0.05
        W = jax.random.normal(k_w, (D, D), dtype=jnp.float32)
        B = jnp.zeros((D,), dtype=jnp.float32)
        return {'z': z, 'dist_matrix': dist_matrix, 'W': W, 'B': B}
    _L0_gnn_all = _L0_gnn_setup()
    _L0_gnn_in = {k: v for k, v in _L0_gnn_all.items() if k in ('W', 'B')}
    del _L0_gnn_all

    def _L1_gnn_setup():
        import jax, jax.numpy as jnp
        import numpy as np
        from jax import lax
        D_MODEL = 128
        D_STATE = 16
        D_CONV = 4
        EXPAND = 2
        D_INNER = EXPAND * D_MODEL
        DT_RANK = (D_MODEL + 15) // 16
        N = 2048
        EPS = 1e-05

        def _mamba(h, w_in, conv_w, conv_b, w_xp, w_dt, b_dt, A_log, D_skip, w_out):
            L = h.shape[0]
            xz = h @ w_in
            xc, z = (xz[:, :D_INNER], xz[:, D_INNER:])
            xpad = jnp.pad(xc, ((D_CONV - 1, 0), (0, 0)))
            xconv = sum((xpad[k:k + L] * conv_w[:, k] for k in range(D_CONV))) + conv_b
            u = jax.nn.silu(xconv)
            dbc = u @ w_xp
            dt = jax.nn.softplus(dbc[:, :DT_RANK] @ w_dt + b_dt)
            B = dbc[:, DT_RANK:DT_RANK + D_STATE]
            C = dbc[:, DT_RANK + D_STATE:]
            A = -jnp.exp(A_log)
            dA = jnp.exp(dt[:, :, None] * A[None])
            dBu = dt[:, :, None] * B[:, None, :] * u[:, :, None]

            def step(hst, inp):
                dAt, dBut, Ct = inp
                hst = dAt * hst + dBut
                return (hst, hst @ Ct)
            _, ys = lax.scan(step, jnp.zeros((D_INNER, D_STATE), h.dtype), (dA, dBu, C))
            y = ys + u * D_skip
            y = y * jax.nn.silu(z)
            return y @ w_out
        key = jax.random.key(seed)
        ks = jax.random.split(key, 16)
        x = jax.random.normal(ks[0], (N, D_MODEL), dtype=jnp.float32)
        a = jax.random.uniform(ks[1], (N, N), dtype=jnp.float32)
        adj = a / a.sum(axis=1, keepdims=True)
        s = lambda fi, fo: 1.0 / np.sqrt(fi)
        gcn_w = jax.random.uniform(ks[2], (D_MODEL, D_MODEL), jnp.float32, -s(D_MODEL, 0), s(D_MODEL, 0))
        gcn_b = jnp.zeros((D_MODEL,), jnp.float32)
        ln_g = jnp.ones((D_MODEL,), jnp.float32)
        ln_b = jnp.zeros((D_MODEL,), jnp.float32)
        w_in = jax.random.normal(ks[3], (D_MODEL, 2 * D_INNER), jnp.float32) * s(D_MODEL, 0)
        conv_w = jax.random.normal(ks[4], (D_INNER, D_CONV), jnp.float32) * s(D_CONV, 0)
        conv_b = jnp.zeros((D_INNER,), jnp.float32)
        w_xp = jax.random.normal(ks[5], (D_INNER, DT_RANK + 2 * D_STATE), jnp.float32) * s(D_INNER, 0)
        w_dt = jax.random.normal(ks[6], (DT_RANK, D_INNER), jnp.float32) * s(DT_RANK, 0)
        b_dt = jnp.log(jnp.expm1(jnp.exp(jax.random.uniform(ks[7], (D_INNER,), jnp.float32, np.log(0.001), np.log(0.1)))))
        A_log = jnp.log(jnp.broadcast_to(jnp.arange(1, D_STATE + 1, dtype=jnp.float32), (D_INNER, D_STATE)))
        D_skip = jnp.ones((D_INNER,), jnp.float32)
        w_out = jax.random.normal(ks[8], (D_INNER, D_MODEL), jnp.float32) * s(D_INNER, 0)
        return dict(x=x, adj=adj, gcn_w=gcn_w, gcn_b=gcn_b, ln_g=ln_g, ln_b=ln_b, w_in=w_in, conv_w=conv_w, conv_b=conv_b, w_xp=w_xp, w_dt=w_dt, b_dt=b_dt, A_log=A_log, D_skip=D_skip, w_out=w_out)
    _L1_gnn_all = _L1_gnn_setup()
    _L1_gnn_in = {k: v for k, v in _L1_gnn_all.items() if k in ('gcn_w', 'gcn_b', 'ln_g', 'ln_b', 'w_in', 'conv_w', 'conv_b', 'w_xp', 'w_dt', 'b_dt', 'A_log', 'D_skip', 'w_out')}
    del _L1_gnn_all
    return {'x': x, 'adj': adj, 'L0_gnn_W': _L0_gnn_in['W'], 'L0_gnn_B': _L0_gnn_in['B'], 'L1_gnn_gcn_w': _L1_gnn_in['gcn_w'], 'L1_gnn_gcn_b': _L1_gnn_in['gcn_b'], 'L1_gnn_ln_g': _L1_gnn_in['ln_g'], 'L1_gnn_ln_b': _L1_gnn_in['ln_b'], 'L1_gnn_w_in': _L1_gnn_in['w_in'], 'L1_gnn_conv_w': _L1_gnn_in['conv_w'], 'L1_gnn_conv_b': _L1_gnn_in['conv_b'], 'L1_gnn_w_xp': _L1_gnn_in['w_xp'], 'L1_gnn_w_dt': _L1_gnn_in['w_dt'], 'L1_gnn_b_dt': _L1_gnn_in['b_dt'], 'L1_gnn_A_log': _L1_gnn_in['A_log'], 'L1_gnn_D_skip': _L1_gnn_in['D_skip'], 'L1_gnn_w_out': _L1_gnn_in['w_out']}

def reference(x, adj, L0_gnn_W, L0_gnn_B, L1_gnn_gcn_w, L1_gnn_gcn_b, L1_gnn_ln_g, L1_gnn_ln_b, L1_gnn_w_in, L1_gnn_conv_w, L1_gnn_conv_b, L1_gnn_w_xp, L1_gnn_w_dt, L1_gnn_b_dt, L1_gnn_A_log, L1_gnn_D_skip, L1_gnn_w_out):
    import jax
    import jax.numpy as jnp

    def _L0_gnn_ref(z, dist_matrix, W, B):
        import jax, jax.numpy as jnp
        import numpy as np
        N = 4096
        D = 128
        CUTOFF = 1.0
        MU = 1.0
        SIGMA = 0.5

        def sensitivity(r, mu, sigma):
            return jnp.exp(-(1.0 / r - 1.0 / mu) ** 2 / (2.0 * sigma * sigma))
        msg = z @ W + B
        sens = sensitivity(dist_matrix, MU, SIGMA)
        weights = jnp.where(dist_matrix < CUTOFF, sens, 0.0)
        return weights @ msg

    def _L1_gnn_ref(x, adj, gcn_w, gcn_b, ln_g, ln_b, w_in, conv_w, conv_b, w_xp, w_dt, b_dt, A_log, D_skip, w_out):
        import jax, jax.numpy as jnp
        import numpy as np
        from jax import lax
        D_MODEL = 128
        D_STATE = 16
        D_CONV = 4
        EXPAND = 2
        D_INNER = EXPAND * D_MODEL
        DT_RANK = (D_MODEL + 15) // 16
        N = 2048
        EPS = 1e-05

        def _mamba(h, w_in, conv_w, conv_b, w_xp, w_dt, b_dt, A_log, D_skip, w_out):
            L = h.shape[0]
            xz = h @ w_in
            xc, z = (xz[:, :D_INNER], xz[:, D_INNER:])
            xpad = jnp.pad(xc, ((D_CONV - 1, 0), (0, 0)))
            xconv = sum((xpad[k:k + L] * conv_w[:, k] for k in range(D_CONV))) + conv_b
            u = jax.nn.silu(xconv)
            dbc = u @ w_xp
            dt = jax.nn.softplus(dbc[:, :DT_RANK] @ w_dt + b_dt)
            B = dbc[:, DT_RANK:DT_RANK + D_STATE]
            C = dbc[:, DT_RANK + D_STATE:]
            A = -jnp.exp(A_log)
            dA = jnp.exp(dt[:, :, None] * A[None])
            dBu = dt[:, :, None] * B[:, None, :] * u[:, :, None]

            def step(hst, inp):
                dAt, dBut, Ct = inp
                hst = dAt * hst + dBut
                return (hst, hst @ Ct)
            _, ys = lax.scan(step, jnp.zeros((D_INNER, D_STATE), h.dtype), (dA, dBu, C))
            y = ys + u * D_skip
            y = y * jax.nn.silu(z)
            return y @ w_out
        h = jax.nn.relu(adj @ x @ gcn_w + gcn_b)
        mu = h.mean(-1, keepdims=True)
        var = h.var(-1, keepdims=True)
        h = (h - mu) * lax.rsqrt(var + EPS) * ln_g + ln_b
        return _mamba(h, w_in, conv_w, conv_b, w_xp, w_dt, b_dt, A_log, D_skip, w_out)
    h = jnp.maximum(_layernorm(x, axis=-1), 0.0)
    x = x + _L0_gnn_ref(h, adj, L0_gnn_W, L0_gnn_B)
    h = jnp.maximum(_layernorm(x, axis=-1), 0.0)
    x = x + _L1_gnn_ref(h, adj, L1_gnn_gcn_w, L1_gnn_gcn_b, L1_gnn_ln_g, L1_gnn_ln_b, L1_gnn_w_in, L1_gnn_conv_w, L1_gnn_conv_b, L1_gnn_w_xp, L1_gnn_w_dt, L1_gnn_b_dt, L1_gnn_A_log, L1_gnn_D_skip, L1_gnn_w_out)
    return x

_drawn_inputs = setup_inputs


def setup_inputs(seed=0):
    import zlib

    import numpy as np

    out = dict(_drawn_inputs(seed))
    spreads = {'L0_gnn_B': (0.0, 0.472),
     'L1_gnn_gcn_b': (0.0, 0.561),
     'L1_gnn_ln_g': (1.0, 0.6),
     'L1_gnn_ln_b': (0.0, 0.8),
     'L1_gnn_conv_b': (0.0, 0.8),
     'L1_gnn_D_skip': (1.0, 0.6)}
    factors = {'L1_gnn_w_xp': 2.875, 'L1_gnn_w_dt': 8.0, 'L1_gnn_b_dt': 8.0, 'L1_gnn_A_log': 2.886}
    for name, (base, spread) in spreads.items():
        noise = np.random.default_rng([zlib.crc32(name.encode()), seed]).standard_normal(out[name].shape)
        drawn = base * np.exp(spread * noise) if base else spread * noise
        out[name] = jnp.asarray(drawn.astype(out[name].dtype))
    for name, factor in factors.items():
        out[name] = (out[name] * factor).astype(out[name].dtype)
    return out
```

```python
from contextlib import ExitStack

import concourse.bass as bass
from concourse import mybir

F32 = mybir.dt.float32
BF16 = mybir.dt.bfloat16
ALU = mybir.AluOpType
ACT = mybir.ActivationFunctionType

P = 128
N = 8192
D = 128
RB = 4
GR = RB * P
G = N // GR
CW = 512
JB = CW // P
K = N // CW
SLOTS = 4
LAG = 3
DI = 256
H = DI // P
S = 16
RANK = 8
TAPS = 4
HIST = TAPS - 1
BC = 2 * S
EPS = 1e-5
TINY = 1e-12
ROWS_AT = 8
PARAMS = 16
BANK = 512
LN_EXP = "natural_log_exp_and_others"


def after(eng, sem, count):
    if not isinstance(count, int) or count > 0:
        eng.wait_ge(sem, count)


class Chain:

    def __init__(self, eng, sem):
        self.eng, self.sem = eng, sem

    def __call__(self, instruction, count):
        instruction.then_inc(self.sem, 1)
        self.eng.wait_ge(self.sem, count)


def variance_steps(nc, stats, mean, var, diff):
    return [
        lambda: nc.vector.tensor_tensor(mean, stats[:, :, 1], stats[:, :, 4], ALU.add),
        lambda: nc.vector.tensor_tensor(diff, stats[:, :, 1], stats[:, :, 4], ALU.subtract),
        lambda: nc.vector.tensor_tensor(var, stats[:, :, 2], stats[:, :, 5], ALU.add),
        lambda: nc.vector.tensor_scalar(mean, mean, 0.5, None, ALU.mult),
        lambda: nc.vector.scalar_tensor_tensor(out=diff, in0=diff, scalar=0.25, in1=diff,
                                               op0=ALU.mult, op1=ALU.mult),
        lambda: nc.vector.scalar_tensor_tensor(out=var, in0=var, scalar=1.0 / D, in1=diff,
                                               op0=ALU.mult, op1=ALU.add),
        lambda: nc.vector.tensor_scalar(var, var, EPS, None, ALU.add),
    ]


VARIANCE = 7


def newton_steps(nc, root, var, work):
    return [
        lambda: nc.vector.tensor_tensor(work, root, root, ALU.mult),
        lambda: nc.vector.tensor_tensor(work, work, var, ALU.mult),
        lambda: nc.vector.tensor_scalar(work, work, -0.5, 1.5, ALU.mult, ALU.add),
        lambda: nc.vector.tensor_tensor(root, root, work, ALU.mult),
    ]


NEWTON = 4


def layer1(nc, ctx, x, adj, w0, b0, out, h2, adj_slot, ident):
    adj_v = adj.rearrange("(g r p) c -> g p r c", r=RB, p=P)
    x_v = x.rearrange("(g r p) d -> g p r d", r=RB, p=P)
    out_v = out.rearrange("(g r p) d -> g p r d", r=RB, p=P)
    x_all = x.rearrange("(b p) d -> p b d", p=P)

    def sb(name, shape, dt=F32):
        return ctx.enter_context(nc.sbuf_tensor(name, shape, dt))

    def sem(name):
        return ctx.enter_context(nc.semaphore(name))

    msg = sb("msg", [P, N // P, D])
    edge = sb("edge", [P, SLOTS, JB * GR])
    w0_sb = sb("w0_sb", [D, D])
    b0_bc = sb("b0_bc", [P, RB, D])
    ht = sb("ht", [D, 2, GR])
    yt = sb("yt", [D, GR])
    x_in = sb("x_in", [P, RB, D])
    x1 = sb("x1", [P, RB, D])
    stats0 = sb("stats0", [P, N // P, 6])
    mean0 = sb("mean0", [P, N // P])
    var0 = sb("var0", [P, N // P])
    root0 = sb("root0", [P, N // P])
    work0 = sb("work0", [P, N // P])
    stats = sb("stats", [P, RB, 6])
    mean = sb("mean", [P, RB])
    var = sb("var", [P, RB])
    root = sb("root", [P, RB])
    work = sb("work", [P, RB])
    tiny = sb("tiny", [P, 1])
    minus2 = sb("minus2", [P, 1])
    ps = ctx.enter_context(nc.psum_tensor("ps_layer1", [P, 8 * BANK], F32))
    turn_ps = ps[:, 0:4 * BANK].rearrange("p (s c) -> p s c", s=2)
    acc = ps[:, 4 * BANK:5 * BANK]
    misc = ps[:, 5 * BANK:6 * BANK]

    consts = sem("consts")
    weights = sem("weights")
    x_here = sem("x_here")
    stats_done = sem("stats_done")
    var_ready = sem("var_ready")
    ln_ready = sem("ln_ready")
    root_ready = sem("root_ready")
    normed = sem("normed")
    h_turned = sem("h_turned")
    ht_ready = sem("ht_ready")
    msg_ps = sem("msg_ps")
    msg_ready = sem("msg_ready")
    adj_here = [sem(f"adj_here{i}") for i in range(SLOTS)]
    masked = sem("masked")
    turned = sem("turned")
    ln_done = sem("ln_done")
    recip_done = sem("recip_done")
    expo_done = sem("expo_done")
    edge_ready = sem("edge_ready")
    mm_done = sem("mm_done")
    yt_ready = sem("yt_ready")
    y_turned = sem("y_turned")
    xg_here = sem("xg_here")
    x1_ready = sem("x1_ready")
    x1_kept = sem("x1_kept")
    v_own = sem("v_own")
    gvar_ready = sem("gvar_ready")
    gln_ready = sem("gln_ready")
    groot_ready = sem("groot_ready")
    h2_ready = sem("h2_ready")

    own = VARIANCE + NEWTON + 2

    with nc.Block() as block:
        @block.sync
        def _(sp):
            sp.dma_start(w0_sb[:, :], w0).then_inc(weights, 16)
            sp.dma_start(b0_bc[:, :, :], b0.rearrange("(o r d) -> o r d", o=1, r=1).to_broadcast([P, RB, D])
                         ).then_inc(weights, 16)
            for q in range(4):
                n = N // P // 4
                sp.dma_start(h2[:, q * n:(q + 1) * n, :], x_all[:, q * n:(q + 1) * n, :]).then_inc(x_here, 16)

            def load(g, k):
                after(sp, turned, 2 * (K * g + k) - 2 * SLOTS + 2)
                sp.dma_start(adj_slot[:, k % SLOTS], adj_v[g, :, :, k * CW:(k + 1) * CW]
                             ).then_inc(adj_here[k % SLOTS], 16)

            def fetch_rows(g):
                after(sp, x1_ready, g)
                sp.dma_start(x_in[:, :, :], x_v[g]).then_inc(xg_here, 16)

            def keep_rows(g):
                sp.wait_ge(x1_ready, g + 1)
                sp.dma_start(out_v[g], x1[:, :, :]).then_inc(x1_kept, 16)

            sp.sem_inc(x1_kept, 16)
            for k in range(K):
                load(0, k)
            fetch_rows(0)
            with sp.Fori(1, G) as g:
                for k in range(K):
                    load(g, k)
                    if k == ROWS_AT:
                        keep_rows(g - 1)
                        fetch_rows(g)
            keep_rows(G - 1)
            sp.wait_ge(x1_kept, 16 * (G + 1))

        @block.gpsimd
        def _(pool):
            nc.gpsimd.memset(ident[:, :], 0.0).then_inc(consts, 1)
            nc.gpsimd.memset(tiny[:, :], TINY).then_inc(consts, 1)
            nc.gpsimd.memset(minus2[:, :], -2.0).then_inc(consts, 1)
            pool.wait_ge(consts, 3)
            nc.gpsimd.affine_select(out=ident[:, :], in_=ident[:, :], compare_op=ALU.not_equal, fill=1.0,
                                    base=0, pattern=[[-1, P]], channel_multiplier=1).then_inc(consts, 1)

        @block.scalar
        def _(act):
            nc.scalar.preload_act_table_set(LN_EXP)
            act.wait_ge(consts, 4)
            act.wait_ge(var_ready, 1)
            nc.scalar.activation(root0[:, :], var0[:, :], ACT.Ln).then_inc(ln_ready, 1)
            act.wait_ge(ln_ready, 1)
            nc.scalar.activation(root0[:, :], root0[:, :], ACT.Exp, scale=-0.5).then_inc(root_ready, 1)

            def relu_turned(i, b):
                act.wait_ge(h_turned, 2 * i + b + 1)
                after(act, msg_ps, 2 * i + b - 1)
                nc.scalar.activation(ht[:, b, :], ps[:, b * BANK:(b + 1) * BANK], ACT.Relu).then_inc(ht_ready, 1)

            for b in range(2):
                relu_turned(0, b)
            with act.Fori(1, G // 2) as i:
                for b in range(2):
                    relu_turned(i, b)

            def weigh(g, k):
                act.wait_ge(expo_done, K * g + k + 1)
                e = edge[:, k % SLOTS, :]
                nc.scalar.activation(e, e, ACT.Exp, scale=-2.0, bias=minus2[:, 0:1]).then_inc(edge_ready, 1)

            def chunk(g, k):
                c = K * g + k
                after(act, mm_done, c - SLOTS + 1)
                for s in range(2):
                    act.wait_ge(turned, 2 * c + s + 1)
                    nc.scalar.activation(edge[:, k % SLOTS, s * 2 * BANK:(s + 1) * 2 * BANK], turn_ps[:, s, :],
                                         ACT.Ln, bias=tiny[:, 0:1]).then_inc(ln_done, 1)
                act.wait_ge(ln_done, 2 * c + 2)
                e = edge[:, k % SLOTS, :]
                nc.scalar.activation(e, e, ACT.Exp, scale=-1.0).then_inc(recip_done, 1)

            def group_root(g):
                act.wait_ge(gvar_ready, g + 1)
                nc.scalar.activation(root[:, :], var[:, :], ACT.Ln).then_inc(gln_ready, 1)
                act.wait_ge(gln_ready, g + 1)
                nc.scalar.activation(root[:, :], root[:, :], ACT.Exp, scale=-0.5).then_inc(groot_ready, 1)

            for k in range(K):
                chunk(0, k)
                if k:
                    weigh(0, k - 1)
            with act.Fori(1, G) as g:
                for k in range(K):
                    chunk(g, k)
                    weigh(g, k - 1)
                    if k == 4:
                        group_root(g - 1)
            weigh(G - 1, K - 1)
            group_root(G - 1)

        @block.vector
        def _(dve):
            chain = Chain(dve, v_own)
            dve.wait_ge(x_here, 64)
            with dve.Fori(0, G) as g:
                for r in range(RB):
                    nc.vector.bn_stats(stats0[:, bass.ds(g * RB + r, 1), :], h2[:, bass.ds(g * RB + r, 1), :]
                                       ).then_inc(stats_done, 1)
            dve.wait_ge(stats_done, N // P)
            *most, last = variance_steps(nc, stats0, mean0[:, :], var0[:, :], work0[:, :])
            for n, step in enumerate(most):
                chain(step(), n + 1)
            last().then_inc(var_ready, 1)
            dve.wait_ge(var_ready, 1)
            dve.wait_ge(root_ready, 1)
            for n, step in enumerate(newton_steps(nc, root0[:, :], var0[:, :], work0[:, :])):
                chain(step(), VARIANCE + n)
            base0 = VARIANCE - 1 + NEWTON

            def norm_rows(i):
                for r in range(RB):
                    b = bass.ds(i * RB + r, 1)
                    blk = h2[:, b, :]
                    ins = nc.vector.tensor_scalar(blk, blk, mean0[:, b], root0[:, b],
                                                  ALU.subtract, ALU.mult)
                ins.then_inc(normed, 1)

            def add_bias(i, b):
                dve.wait_ge(msg_ps, 2 * i + b + 1)
                nc.vector.tensor_tensor(msg[:, bass.ds(RB * (2 * i + b), RB), :],
                                        ps[:, (2 + b) * BANK:(3 + b) * BANK].rearrange("p (r d) -> p r d", r=RB),
                                        b0_bc[:, :, :], ALU.add).then_inc(msg_ready, 1)

            with dve.Fori(0, G) as i:
                norm_rows(i)
            dve.wait_ge(weights, 32)
            with dve.Fori(0, G // 2) as i:
                for b in range(2):
                    add_bias(i, b)

            def mask(g, k):
                dve.wait_ge(adj_here[k % SLOTS], 16 * (K // SLOTS * g + k // SLOTS + 1))
                a = adj_slot[:, k % SLOTS]
                nc.vector.scalar_tensor_tensor(out=a, in0=a, scalar=1.0, in1=a, op0=ALU.is_lt, op1=ALU.mult
                                               ).then_inc(masked, 1)

            def exponent(g, k):
                dve.wait_ge(recip_done, K * g + k + 1)
                e = edge[:, k % SLOTS, :]
                nc.vector.scalar_tensor_tensor(out=e, in0=e, scalar=2.0, in1=e, op0=ALU.subtract, op1=ALU.mult
                                               ).then_inc(expo_done, 1)

            def take_y(g):
                dve.wait_ge(mm_done, K * (g + 1))
                nc.vector.tensor_copy(yt[:, :], acc).then_inc(yt_ready, 1)

            def first_half(g):
                o = base0 + own * g
                dve.wait_ge(y_turned, g + 1)
                dve.wait_ge(xg_here, 16 * (g + 1))
                dve.wait_ge(x1_kept, 16 * (g + 1))
                nc.vector.tensor_tensor(x1[:, :, :], misc.rearrange("p (r d) -> p r d", r=RB), x_in[:, :, :], ALU.add
                                        ).then_inc(x1_ready, 1)
                dve.wait_ge(x1_ready, g + 1)
                for r in range(RB):
                    ins = nc.vector.bn_stats(stats[:, r, :], x1[:, r, :])
                chain(ins, o + 1)
                *most, last = variance_steps(nc, stats, mean[:, :], var[:, :], work[:, :])
                for n, step in enumerate(most):
                    chain(step(), o + 2 + n)
                last().then_inc(gvar_ready, 1)

            def second_half(g):
                o = base0 + own * g + VARIANCE
                dve.wait_ge(groot_ready, g + 1)
                dve.wait_ge(gvar_ready, g + 1)
                for n, step in enumerate(newton_steps(nc, root[:, :], var[:, :], work[:, :])):
                    chain(step(), o + 1 + n)
                for r in range(RB):
                    ins = nc.vector.tensor_scalar(x_norm(g, r), x1[:, r, :], mean[:, r:r + 1], root[:, r:r + 1],
                                                  ALU.subtract, ALU.mult)
                chain(ins, o + 1 + NEWTON)
                blk = h2[:, bass.ds(RB * g, RB), :]
                chain(nc.vector.tensor_scalar(blk, blk, 0.0, None, ALU.max), o + 2 + NEWTON)

            def x_norm(g, r):
                return h2[:, bass.ds(RB * g + r, 1), :]

            for k in range(K):
                mask(0, k)
                if k:
                    exponent(0, k - 1)
            with dve.Fori(1, G) as g:
                for k in range(K):
                    mask(g, k)
                    exponent(g, k - 1)
                    if k == LAG - 1:
                        take_y(g - 1)
                    if k == LAG + 1:
                        first_half(g - 1)
                    if k == 6:
                        second_half(g - 1)
            exponent(G - 1, K - 1)
            take_y(G - 1)
            first_half(G - 1)
            second_half(G - 1)

        @block.tensor
        def _(pe):
            pe.wait_ge(consts, 4)
            pe.wait_ge(weights, 32)

            def turn_rows(i, b):
                after(pe, ht_ready, 2 * i + b - 1)
                for r in range(RB):
                    ins = nc.tensor.transpose(ps[:, b * BANK + r * P:b * BANK + (r + 1) * P],
                                              h2[:, (2 * i + b) * RB + r, :], ident[:, :])
                ins.then_inc(h_turned, 1)

            def message(i, b):
                pe.wait_ge(ht_ready, 2 * i + b + 1)
                after(pe, msg_ready, 2 * i + b - 1)
                for r in range(RB):
                    ins = nc.tensor.matmul(ps[:, (2 + b) * BANK + r * D:(2 + b) * BANK + (r + 1) * D],
                                           ht[:, b, r * P:(r + 1) * P], w0_sb[:, :], start=True, stop=True)
                ins.then_inc(msg_ps, 1)

            for i in range(G // 2):
                for b in range(2):
                    pe.wait_ge(normed, 2 * i + b + 1)
                    turn_rows(i, b)
                    message(i, b)

            pe.wait_ge(msg_ready, G)

            def turn(g, k):
                c = K * g + k
                pe.wait_ge(masked, c + 1)
                for s in range(2):
                    after(pe, ln_done, 2 * c + s - 1)
                    for b in range(2):
                        for r in range(RB):
                            ins = nc.tensor.transpose(turn_ps[:, s, b * GR + r * P:b * GR + (r + 1) * P],
                                                      adj_slot[:, k % SLOTS, r, (2 * s + b) * P:(2 * s + b + 1) * P],
                                                      ident[:, :])
                    ins.then_inc(turned, 1)

            def multiply(g, k):
                pe.wait_ge(edge_ready, K * g + k + 1)
                if k == 0:
                    after(pe, yt_ready, g)
                for b in range(JB):
                    j = k * JB + b
                    ins = nc.tensor.matmul(acc, msg[:, j, :], edge[:, k % SLOTS, b * GR:(b + 1) * GR],
                                           start=(j == 0), stop=(j == N // P - 1))
                ins.then_inc(mm_done, 1)

            def turn_y(g):
                pe.wait_ge(yt_ready, g + 1)
                for r in range(RB):
                    ins = nc.tensor.transpose(misc[:, r * P:(r + 1) * P], yt[:, r * P:(r + 1) * P], ident[:, :])
                ins.then_inc(y_turned, 1)

            for k in range(K):
                turn(0, k)
                if k >= LAG:
                    multiply(0, k - LAG)
            with pe.Fori(1, G) as g:
                for k in range(K):
                    turn(g, k)
                    if k >= LAG:
                        multiply(g, k - LAG)
                    else:
                        multiply(g - 1, K + k - LAG)
                    if k == LAG:
                        turn_y(g - 1)
            for k in range(K - LAG, K):
                multiply(G - 1, k)
            turn_y(G - 1)


def layer2(nc, ctx, adj, gcn_w, gcn_b, ln_g, ln_b, w_in, conv_w, conv_b, w_xp, w_dt, b_dt, a_log, d_skip, w_out,
           out, h2, adj_slot, ident):
    adj_v = adj.rearrange("(g r p) c -> g p r c", r=RB, p=P)
    out_v = out.rearrange("(g r p) d -> g p r d", r=RB, p=P)

    def sb(name, shape, dt=F32):
        return ctx.enter_context(nc.sbuf_tensor(name, shape, dt))

    def sem(name):
        return ctx.enter_context(nc.semaphore(name))

    gcn_w_sb = sb("gcn_w_sb", [D, D])
    gcn_b_row = sb("gcn_b_row", [1, D])
    ones_row = sb("ones_row", [1, P])
    ln_g_sb = sb("ln_g_sb", [D, 1])
    ln_b_sb = sb("ln_b_sb", [D, 1])
    w_in_sb = sb("w_in_sb", [D, 2 * DI])
    conv_w_sb = sb("conv_w_sb", [P, H, TAPS])
    conv_b_sb = sb("conv_b_sb", [P, H])
    w_xp_sb = sb("w_xp_sb", [P, H, 3 * BC + RANK])
    w_dt_sb = sb("w_dt_sb", [3 * BC + RANK, DI])
    b_dt_sb = sb("b_dt_sb", [P, H])
    a_sb = sb("a_sb", [P, H, S])
    d_sb = sb("d_sb", [P, H])
    w_out_sb = sb("w_out_sb", [P, H, D])
    one = sb("one", [P, 1])
    pick = sb("pick", [3 * BC, BC, P], BF16)

    turned_adj = sb("turned_adj", [P, 2, JB * GR])
    at = sb("at", [P, GR])
    hn = sb("hn", [P, RB, D])
    ht = sb("ht2", [D, GR])
    stats = sb("stats2", [P, RB, 6])
    mean = sb("mean2", [P, RB])
    var = sb("var2", [P, RB])
    root = sb("root2", [P, RB])
    work = sb("work2", [P, RB])
    xc = sb("xc", [P, H, HIST + GR])
    conv = sb("conv", [P, H, GR])
    zr = sb("zr", [P, H, GR])
    sig = sb("sig", [P, H, GR])
    u = sb("u", [P, H, GR])
    low = sb("low", [P, H, GR])
    rest = hn.rearrange("p r d -> p (r d)")
    dtr = at
    dt = sb("dt", [P, 2, H, GR])
    dtu = sb("dtu", [P, 2, H, GR])
    bcs = sb("bcs", [3 * BC, 2, GR], BF16)
    y = sb("y", [P, 2, H, GR])
    sz = sb("sz", [P, 2, H, GR])
    da = sb("da", [P, 2, H, GR])
    dbu = sb("dbu", [P, 2, H, GR])
    hs = sb("hs", [P, 2, H, GR])
    hc = sb("hc", [P, 2, H, GR])
    state = sb("state", [P, S, H])
    x1g = sb("x1g", [P, RB, D])
    og = sb("og", [P, RB, D])

    ps = ctx.enter_context(nc.psum_tensor("ps_layer2", [P, 8 * BANK], F32))

    def bank(n):
        return ps[:, n * BANK:(n + 1) * BANK]

    acc, misc = bank(2), bank(3)
    b_ps, c_ps = [bank(4), bank(5)], [bank(6), bank(7)]

    params = sem("params")
    consts = sem("consts2")
    a_exp = sem("a_exp")
    a_ready = sem("a_ready")
    adj_here = [sem(f"adj2_here{i}") for i in range(SLOTS)]
    turned = sem("turned2")
    kept = sem("kept2")
    mm_done = sem("mm2_done")
    at_ready = sem("at_ready")
    gcn_ps = sem("gcn_ps")
    gcn_relu = sem("gcn_relu")
    v_own = sem("v_own2")
    var_ready = sem("var2_ready")
    ln_ready = sem("ln2_ready")
    root_ready = sem("root2_ready")
    hn_ready = sem("hn_ready")
    hn_turned = sem("hn_turned")
    ht_ready = sem("ht2_ready")
    hist_ready = sem("hist_ready")
    xz_ps = sem("xz_ps")
    xz_ready = sem("xz_ready")
    conv_done = sem("conv_done")
    a_own = sem("a_own")
    sig_u = sem("sig_u")
    sig_z = sem("sig_z")
    u_ready = sem("u_ready")
    sz_ready = sem("sz_ready")
    y_start = sem("y_start")
    xp_ps = sem("xp_ps")
    xp_read = sem("xp_read")
    bcs_ready = sem("bcs_ready")
    dt_ps = sem("dt_ps")
    dt_arg = sem("dt_arg")
    soft_ready = sem("soft_ready")
    dt_ready = sem("dt_ready")
    dtu_ready = sem("dtu_ready")
    bc_ps = sem("bc_ps")
    da_ready = sem("da_ready")
    dbu_ready = sem("dbu_ready")
    scanned = sem("scanned")
    hc_ready = sem("hc_ready")
    y_added = sem("y_added")
    state_kept = sem("state_kept")
    y_gated = sem("y_gated")
    out_ps = sem("out_ps")
    og_ready = sem("og_ready")
    x1g_here = sem("x1g_here")
    og_kept = sem("og_kept")

    NORM, CONV, SPLIT, SOFT = 1 + VARIANCE - 1 + NEWTON, H * TAPS, 5, 3
    OWN = NORM + CONV + SPLIT + SOFT
    A_OWN = 6

    def walk(body, eng):
        for g in range(3):
            body(g, g % 2)
        with eng.Fori(3, G - 1, 2) as g:
            body(g, 1)
            body(g + 1, 0)
        for g in range(G - 1, G + 3):
            body(g, g % 2)

    def product_in(g):
        return not isinstance(g, int) or g < G

    def prep_in(g):
        return not isinstance(g, int) or 1 <= g <= G

    def items_in(g):
        return not isinstance(g, int) or 2 <= g <= G + 1

    def final_in(g):
        return not isinstance(g, int) or 3 <= g <= G + 2

    with nc.Block() as block:
        @block.sync
        def _(sp):
            def col(v):
                return v.rearrange("(h p) -> p h", p=P)

            b, dtc = w_xp[:, RANK:], w_xp[:, 0:RANK]
            loads = [
                (gcn_w_sb[:, :], gcn_w),
                (ln_g_sb[:, :], ln_g.rearrange("(p o) -> p o", o=1)),
                (ln_b_sb[:, :], ln_b.rearrange("(p o) -> p o", o=1)),
                (w_in_sb[:, :], w_in),
                (conv_w_sb[:, :, :], conv_w.rearrange("(h p) t -> p h t", p=P)),
                (w_dt_sb[3 * BC:3 * BC + RANK, :], w_dt),
                (a_sb[:, :, :], a_log.rearrange("(h p) s -> p h s", p=P)),
                (w_out_sb[:, :, :], w_out.rearrange("(h p) d -> p h d", p=P)),
                (w_xp_sb[:, :, 3 * BC:], dtc.rearrange("(h p) c -> p h c", p=P)),
            ]
            loads += [(w_xp_sb[:, :, q * BC:(q + 1) * BC], b.rearrange("(h p) c -> p h c", p=P)) for q in range(3)]
            loads += [(gcn_b_row[:, :], gcn_b.rearrange("(o d) -> o d", o=1))]
            assert len(loads) + 3 == PARAMS
            for dst, src in loads:
                sp.dma_start(dst, src).then_inc(params, 16)
            with nc.allow_non_contiguous_dma(reason="three short vectors, channels to partitions"):
                sp.dma_start(conv_b_sb[:, :], col(conv_b)).then_inc(params, 16)
                sp.dma_start(b_dt_sb[:, :], col(b_dt)).then_inc(params, 16)
                sp.dma_start(d_sb[:, :], col(d_skip)).then_inc(params, 16)

            def body(g, par):
                for k in range(K):
                    if product_in(g):
                        after(sp, turned, JB * (K * g + k - SLOTS + 1))
                        sp.dma_start(adj_slot[:, k % SLOTS], adj_v[g, :, :, k * CW:(k + 1) * CW]
                                     ).then_inc(adj_here[k % SLOTS], 16)
                    if k == ROWS_AT and final_in(g):
                        sp.wait_ge(og_ready, g - 2)
                        sp.dma_start(out_v[g - 3], og[:, :, :]).then_inc(og_kept, 16)
                    if k == ROWS_AT and final_in(g + 1):
                        after(sp, og_ready, g - 2)
                        sp.dma_start(x1g[:, :, :], out_v[g - 2]).then_inc(x1g_here, 16)

            sp.sem_inc(og_kept, 16)
            walk(body, sp)
            sp.wait_ge(og_kept, 16 * (G + 1))

        @block.gpsimd
        def _(pool):
            nc.gpsimd.memset(one[:, :], 1.0).then_inc(consts, 1)
            nc.gpsimd.memset(ones_row[:, :], 1.0).then_inc(consts, 1)
            nc.gpsimd.memset(state[:, :, :], 0.0).then_inc(consts, 1)
            nc.gpsimd.memset(xc[:, :, GR:], 0.0).then_inc(consts, 1)
            nc.gpsimd.memset(pick[:, :, :], 0.0).then_inc(consts, 1)
            pool.wait_ge(consts, 5)
            for q in range(3):
                nc.gpsimd.affine_select(out=pick[:, :, :], in_=pick[:, :, :], compare_op=ALU.not_equal, fill=1.0,
                                        base=-BC * q, pattern=[[-1, BC], [0, P]], channel_multiplier=1
                                        ).then_inc(consts, 1)
                pool.wait_ge(consts, 6 + q)

            def body(g, par):
                for k in range(K):
                    if k == 1 and prep_in(g):
                        after(pool, conv_done, H * (g - 1))
                        last = xc[:, :, GR:GR + HIST]
                        nc.gpsimd.tensor_tensor(xc[:, :, 0:HIST], last, ones3, ALU.mult).then_inc(hist_ready, 1)
                    if k == 0 and final_in(g):
                        v = y[:, 1 - par]
                        pool.wait_ge(y_added, K * (g - 2))
                        pool.wait_ge(sz_ready, g - 2)
                        nc.gpsimd.tensor_tensor(v, v, sz[:, 1 - par], ALU.mult).then_inc(y_gated, 1)
                    if items_in(g):
                        m = K * (g - 2) + k
                        v = y[:, par]
                        pool.wait_ge(hc_ready, m + 1)
                        if k:
                            pool.wait_ge(y_added, m)
                        else:
                            pool.wait_ge(y_start, H * (g - 1))
                        nc.gpsimd.tensor_tensor(v, v, hc[:, k % 2], ALU.add).then_inc(y_added, 1)
                        nc.gpsimd.tensor_copy(state[:, k, :], hs[:, k % 2, :, GR - 1]).then_inc(state_kept, 1)
                    if k == 12 and prep_in(g):
                        pool.wait_ge(u_ready, g)
                        after(pool, out_ps, g - 2)
                        for h in range(H):
                            nc.gpsimd.tensor_tensor(y[:, 1 - par, h, :], u[:, h, :],
                                                    d_sb[:, h:h + 1].to_broadcast([P, GR]), ALU.mult
                                                    ).then_inc(y_start, 1)

            ones3 = one[:, 0:1].rearrange("p (a b) -> p a b", a=1).to_broadcast([P, H, HIST])
            pool.wait_ge(params, 16 * PARAMS)
            walk(body, pool)

        @block.scalar
        def _(act):
            nc.scalar.preload_act_table_set(LN_EXP)
            act.wait_ge(params, 16 * PARAMS)
            act.wait_ge(consts, 8)
            nc.scalar.activation(a_sb[:, :, :], a_sb[:, :, :], ACT.Exp).then_inc(a_exp, 1)
            act.wait_ge(a_ready, 1)

            def sigmoid(src, n, g, done):
                o = A_OWN * (g - 1) + n
                nc.scalar.activation(sig[:, :, :], src, ACT.Exp, scale=-1.0).then_inc(a_own, 1)
                act.wait_ge(a_own, o + 1)
                nc.scalar.activation(sig[:, :, :], sig[:, :, :], ACT.Ln, bias=one[:, 0:1]).then_inc(a_own, 1)
                act.wait_ge(a_own, o + 2)
                nc.scalar.activation(sig[:, :, :], sig[:, :, :], ACT.Exp, scale=-1.0).then_inc(done, 1)

            def prep(g, par, k):
                if k == 1:
                    act.wait_ge(mm_done, K * g)
                    after(act, dt_ps, H * (g - 1))
                    nc.scalar.activation(at[:, :], acc, ACT.Identity).then_inc(at_ready, 1)
                if k == 2:
                    act.wait_ge(gcn_ps, g)
                    after(act, bcs_ready, g - 1)
                    nc.scalar.activation(hn[:, :, :], misc.rearrange("p (r d) -> p r d", r=RB), ACT.Relu
                                         ).then_inc(gcn_relu, 1)
                if k == 3:
                    act.wait_ge(var_ready, g)
                    nc.scalar.activation(root[:, :], var[:, :], ACT.Ln).then_inc(ln_ready, 1)
                    act.wait_ge(ln_ready, g)
                    nc.scalar.activation(root[:, :], root[:, :], ACT.Exp, scale=-0.5).then_inc(root_ready, 1)
                if k == 5:
                    act.wait_ge(hn_turned, g)
                    after(act, xz_ps, 4 * (g - 1))
                    nc.scalar.activation(ht[:, :], misc, ACT.Identity, scale=ln_g_sb[:, 0:1], bias=ln_b_sb[:, 0:1]
                                         ).then_inc(ht_ready, 1)
                if k in (6, 7, 8, 9):
                    q = k - 6
                    act.wait_ge(xz_ps, 4 * (g - 1) + q + 1)
                    if q == 0:
                        act.wait_ge(hist_ready, g)
                    if q == 2:
                        after(act, dt_ready, g - 1)
                    dst = xc[:, q, HIST:] if q < H else zr[:, q - H, :]
                    nc.scalar.activation(dst, misc, ACT.Identity).then_inc(xz_ready, 1)
                if k == 10:
                    act.wait_ge(conv_done, H * g)
                    after(act, dt_ready, g - 1)
                    sigmoid(conv[:, :, :], 0, g, sig_u)
                if k == 11:
                    act.wait_ge(u_ready, g)
                    act.wait_ge(xz_ready, 4 * g)
                    sigmoid(zr[:, :, :], 2, g, sig_z)
                if k in (13, 14):
                    h = k - 13
                    act.wait_ge(dt_ps, H * (g - 1) + h + 1)
                    nc.scalar.activation(conv[:, h, :], misc, ACT.Identity, bias=b_dt_sb[:, h:h + 1]
                                         ).then_inc(dt_arg, 1)
                if k == 14:
                    o = A_OWN * (g - 1) + 4
                    act.wait_ge(dt_arg, H * g)
                    act.wait_ge(sz_ready, g)
                    nc.scalar.activation(sig[:, :, :], conv[:, :, :], ACT.Abs).then_inc(a_own, 1)
                    act.wait_ge(a_own, o + 1)
                    nc.scalar.activation(sig[:, :, :], sig[:, :, :], ACT.Exp, scale=-1.0).then_inc(a_own, 1)
                    act.wait_ge(a_own, o + 2)
                    nc.scalar.activation(zr[:, :, :], sig[:, :, :], ACT.Ln, bias=one[:, 0:1]).then_inc(soft_ready, 1)

            def body(g, par):
                for k in range(K):
                    if prep_in(g):
                        prep(g, par, k)
                    if product_in(g):
                        after(act, mm_done, K * g + k - 1)
                        for b in range(JB):
                            act.wait_ge(turned, JB * (K * g + k) + b + 1)
                            nc.scalar.activation(turned_adj[:, k % 2, b * GR:(b + 1) * GR], bank(b % 2), ACT.Identity
                                                 ).then_inc(kept, 1)
                    if items_in(g):
                        m = K * (g - 2) + k
                        after(act, scanned, H * (m - 1))
                        if k == 0:
                            act.wait_ge(dt_ready, g - 1)
                        for h in range(H):
                            nc.scalar.activation(da[:, k % 2, h, :], dt[:, par, h, :], ACT.Exp,
                                                 scale=a_sb[:, h, k:k + 1]).then_inc(da_ready, 1)

            walk(body, act)

        @block.vector
        def _(dve):
            chain = Chain(dve, v_own)
            dve.wait_ge(params, 16 * PARAMS)
            dve.wait_ge(consts, 8)
            dve.wait_ge(a_exp, 1)
            nc.vector.tensor_scalar(a_sb[:, :, :], a_sb[:, :, :], -1.0, None, ALU.mult).then_inc(a_ready, 1)

            def prep(g, par, k):
                o = OWN * (g - 1)
                if k == 2:
                    dve.wait_ge(gcn_relu, g)
                    for r in range(RB):
                        ins = nc.vector.bn_stats(stats[:, r, :], hn[:, r, :])
                    chain(ins, o + 1)
                    *most, last = variance_steps(nc, stats, mean[:, :], var[:, :], work[:, :])
                    for n, step in enumerate(most):
                        chain(step(), o + 2 + n)
                    last().then_inc(var_ready, 1)
                if k == 3:
                    dve.wait_ge(var_ready, g)
                    dve.wait_ge(root_ready, g)
                    for n, step in enumerate(newton_steps(nc, root[:, :], var[:, :], work[:, :])):
                        chain(step(), o + VARIANCE + 1 + n)
                    for r in range(RB):
                        ins = nc.vector.tensor_scalar(hn[:, r, :], hn[:, r, :], mean[:, r:r + 1], root[:, r:r + 1],
                                                      ALU.subtract, ALU.mult)
                    ins.then_inc(hn_ready, 1)
                o += NORM
                if k in (8, 9):
                    h = k - 8
                    dve.wait_ge(xz_ready, 4 * (g - 1) + h + 1)
                    dve.wait_ge(hist_ready, g)
                    after(dve, dt_ready, g - 1)
                    nc_first = nc.vector.tensor_scalar(conv[:, h, :], xc[:, h, 0:GR], conv_w_sb[:, h, 0:1],
                                                       conv_b_sb[:, h:h + 1], ALU.mult, ALU.add)
                    chain(nc_first, o + TAPS * h + 1)
                    for t in range(1, TAPS):
                        ins = nc.vector.scalar_tensor_tensor(out=conv[:, h, :], in0=xc[:, h, t:t + GR],
                                                             scalar=conv_w_sb[:, h, t:t + 1], in1=conv[:, h, :],
                                                             op0=ALU.mult, op1=ALU.add)
                        if t < TAPS - 1:
                            chain(ins, o + TAPS * h + 1 + t)
                        else:
                            ins.then_inc(conv_done, 1)
                            dve.wait_ge(conv_done, H * (g - 1) + h + 1)
                            dve.sem_inc(v_own, 1)
                o += CONV
                if k == 10:
                    dve.wait_ge(sig_u, g)
                    after(dve, dtu_ready, g - 1)
                    after(dve, y_start, H * (g - 1))
                    nc.vector.tensor_tensor(u[:, :, :], conv[:, :, :], sig[:, :, :], ALU.mult).then_inc(u_ready, 1)
                if k == 11:
                    dve.wait_ge(sig_z, g)
                    after(dve, y_gated, g - 2)
                    nc.vector.tensor_tensor(sz[:, 1 - par], zr[:, :, :], sig[:, :, :], ALU.mult).then_inc(sz_ready, 1)
                if k == 12:
                    full, parts = misc[0:3 * BC, :], bcs[:, 1 - par, :]
                    dve.wait_ge(xp_ps, g)
                    after(dve, bc_ps, K * (g - 2))
                    nc.vector.tensor_copy(dtr[3 * BC:3 * BC + RANK, :], misc[3 * BC:3 * BC + RANK, :]
                                          ).then_inc(xp_read, 1)
                    chain(nc.vector.tensor_copy(parts, full), o + 1)
                    nc.vector.tensor_tensor(rest[0:3 * BC, :], full, parts, ALU.subtract).then_inc(xp_read, 1)
                    dve.wait_ge(xp_read, 2 * g)
                    chain(nc.vector.tensor_copy(parts[BC:2 * BC, :], rest[BC:2 * BC, :]), o + 2)
                    chain(nc.vector.tensor_copy(parts[2 * BC:, :], rest[2 * BC:3 * BC, :]), o + 3)
                    chain(nc.vector.tensor_tensor(rest[2 * BC:3 * BC, :], rest[2 * BC:3 * BC, :], parts[2 * BC:, :],
                                                  ALU.subtract), o + 4)
                    chain(nc.vector.tensor_copy(parts[2 * BC:, :], rest[2 * BC:3 * BC, :]), o + 5)
                    dve.sem_inc(bcs_ready, 1)
                o += SPLIT
                if k == 15:
                    dve.wait_ge(soft_ready, g)
                    chain(nc.vector.tensor_scalar(low[:, :, :], sig[:, :, :], 1.0, 1.0, ALU.add, ALU.subtract), o + 1)
                    chain(nc.vector.tensor_tensor(low[:, :, :], sig[:, :, :], low[:, :, :], ALU.subtract), o + 2)
                    chain(nc.vector.tensor_tensor(low[:, :, :], low[:, :, :], zr[:, :, :], ALU.add), o + 3)
                    after(dve, da_ready, H * K * (g - 2))
                    nc.vector.scalar_tensor_tensor(out=dt[:, 1 - par], in0=conv[:, :, :], scalar=0.0,
                                                   in1=low[:, :, :], op0=ALU.max, op1=ALU.add).then_inc(dt_ready, 1)
                    dve.wait_ge(dt_ready, g)
                    after(dve, dbu_ready, K * (g - 2))
                    nc.vector.tensor_tensor(dtu[:, 1 - par], dt[:, 1 - par], u[:, :, :], ALU.mult
                                            ).then_inc(dtu_ready, 1)

            def item(g, par, k):
                m = K * (g - 2) + k
                b = k % 2
                dve.wait_ge(bc_ps, m + 1)
                dve.wait_ge(dtu_ready, g - 1)
                after(dve, scanned, H * (m - 1))
                nc.vector.tensor_tensor(dbu[:, b], dtu[:, par],
                                        b_ps[b].rearrange("p (o t) -> p o t", o=1).to_broadcast([P, H, GR]), ALU.mult
                                        ).then_inc(dbu_ready, 1)
                dve.wait_ge(dbu_ready, m + 1)
                dve.wait_ge(da_ready, H * (m + 1))
                if k == 0:
                    after(dve, state_kept, K * (g - 2))
                after(dve, state_kept, m - 1)
                after(dve, hc_ready, m - 1)
                for h in range(H):
                    nc.vector.tensor_tensor_scan(hs[:, b, h, :], da[:, b, h, :], dbu[:, b, h, :],
                                                 state[:, k, h:h + 1], ALU.mult, ALU.add).then_inc(scanned, 1)
                dve.wait_ge(scanned, H * (m + 1))
                after(dve, y_added, m - 1)
                nc.vector.tensor_tensor(hc[:, b], hs[:, b],
                                        c_ps[b].rearrange("p (o t) -> p o t", o=1).to_broadcast([P, H, GR]), ALU.mult
                                        ).then_inc(hc_ready, 1)

            def body(g, par):
                for k in range(K):
                    if k == 3 and final_in(g):
                        dve.wait_ge(out_ps, g - 2)
                        dve.wait_ge(x1g_here, 16 * (g - 2))
                        dve.wait_ge(og_kept, 16 * (g - 2))
                        nc.vector.tensor_tensor(og[:, :, :], misc.rearrange("p (r d) -> p r d", r=RB), x1g[:, :, :],
                                                ALU.add).then_inc(og_ready, 1)
                    if items_in(g):
                        item(g, par, k)
                    if prep_in(g):
                        prep(g, par, k)

            walk(body, dve)

        @block.tensor
        def _(pe):
            pe.wait_ge(params, 16 * PARAMS)
            pe.wait_ge(consts, 8)

            def turn(g, k, b):
                n = JB * (K * g + k) + b
                if b == 0:
                    pe.wait_ge(adj_here[k % SLOTS], 16 * (K // SLOTS * g + k // SLOTS + 1))
                after(pe, kept, n - 1)
                for r in range(RB):
                    ins = nc.tensor.transpose(bank(b % 2)[:, r * P:(r + 1) * P],
                                              adj_slot[:, k % SLOTS, r, b * P:(b + 1) * P], ident[:, :])
                ins.then_inc(turned, 1)

            def multiply(g, k, b):
                j = k * JB + b
                pe.wait_ge(kept, JB * (K * g + k) + b + 1)
                if j == 0:
                    after(pe, at_ready, g)
                ins = nc.tensor.matmul(acc, h2[:, j, :], turned_adj[:, k % 2, b * GR:(b + 1) * GR],
                                       start=(j == 0), stop=(j == N // P - 1))
                if b == JB - 1:
                    ins.then_inc(mm_done, 1)

            def prep(g, par, k):
                if k == 1:
                    pe.wait_ge(at_ready, g)
                    after(pe, dt_arg, H * (g - 1))
                    for r in range(RB):
                        part = misc[:, r * D:(r + 1) * D]
                        nc.tensor.matmul(part, ones_row[:, :], gcn_b_row[:, :], start=True, stop=False)
                        ins = nc.tensor.matmul(part, at[:, r * P:(r + 1) * P], gcn_w_sb[:, :],
                                               start=False, stop=True)
                    ins.then_inc(gcn_ps, 1)
                if k == 4:
                    pe.wait_ge(hn_ready, g)
                    pe.wait_ge(gcn_relu, g)
                    for r in range(RB):
                        ins = nc.tensor.transpose(misc[:, r * P:(r + 1) * P], hn[:, r, :], ident[:, :])
                    ins.then_inc(hn_turned, 1)
                if k in (5, 6, 7, 8):
                    q = k - 5
                    pe.wait_ge(ht_ready, g)
                    if q:
                        pe.wait_ge(xz_ready, 4 * (g - 1) + q)
                    nc.tensor.matmul(misc, w_in_sb[:, q * P:(q + 1) * P], ht[:, :], start=True, stop=True
                                     ).then_inc(xz_ps, 1)
                if k == 11:
                    pe.wait_ge(u_ready, g)
                    pe.wait_ge(xz_ready, 4 * g)
                    for h in range(H):
                        ins = nc.tensor.matmul(misc[0:3 * BC + RANK, :], w_xp_sb[:, h, :], u[:, h, :],
                                               start=(h == 0), stop=(h == H - 1))
                    ins.then_inc(xp_ps, 1)
                if k in (12, 13):
                    h = k - 12
                    pe.wait_ge(xp_read, 2 * g)
                    if h:
                        pe.wait_ge(dt_arg, H * (g - 1) + h)
                    nc.tensor.matmul(misc, w_dt_sb[3 * BC:3 * BC + RANK, h * P:(h + 1) * P],
                                     dtr[3 * BC:3 * BC + RANK, :], start=True, stop=True).then_inc(dt_ps, 1)

            def spread(g, par, k):
                m = K * (g - 2) + k
                if k == 0:
                    pe.wait_ge(bcs_ready, g - 1)
                after(pe, hc_ready, m - 1)
                nc.tensor.matmul(b_ps[k % 2], pick[:, k, :], bcs[:, par, :], start=True, stop=True)
                nc.tensor.matmul(c_ps[k % 2], pick[:, S + k, :], bcs[:, par, :], start=True, stop=True
                                 ).then_inc(bc_ps, 1)

            def body(g, par):
                for k in range(K):
                    if items_in(g):
                        spread(g, par, k)
                    for b in range(JB):
                        if product_in(g):
                            turn(g, k, b)
                        if b % 2:
                            for q in (b - 1, b):
                                if k and product_in(g):
                                    multiply(g, k - 1, q)
                                if k == 0 and prep_in(g):
                                    multiply(g - 1, K - 1, q)
                    if prep_in(g):
                        prep(g, par, k)
                    if k == 2 and final_in(g):
                        v = y[:, 1 - par]
                        pe.wait_ge(y_gated, g - 2)
                        if prep_in(g):
                            pe.wait_ge(gcn_relu, g)
                        else:
                            pe.wait_ge(dt_arg, H * G)
                            after(pe, og_ready, g - 3)
                        for r in range(RB):
                            for h in range(H):
                                ins = nc.tensor.matmul(misc[:, r * D:(r + 1) * D], v[:, h, r * P:(r + 1) * P],
                                                       w_out_sb[:, h, :], start=(h == 0), stop=(h == H - 1))
                        ins.then_inc(out_ps, 1)
                    if k == 3 and final_in(g) and prep_in(g):
                        pe.wait_ge(og_ready, g - 2)

            walk(body, pe)


def build(nc, x, adj, L0_gnn_W, L0_gnn_B, L1_gnn_gcn_w, L1_gnn_gcn_b, L1_gnn_ln_g, L1_gnn_ln_b, L1_gnn_w_in,
          L1_gnn_conv_w, L1_gnn_conv_b, L1_gnn_w_xp, L1_gnn_w_dt, L1_gnn_b_dt, L1_gnn_A_log, L1_gnn_D_skip,
          L1_gnn_w_out, out):
    with ExitStack() as both:
        h2 = both.enter_context(nc.sbuf_tensor("h2", [P, N // P, D], F32))
        adj_slot = both.enter_context(nc.sbuf_tensor("adj_slot", [P, SLOTS, RB, CW], F32))
        ident = both.enter_context(nc.sbuf_tensor("ident", [P, P], F32))
        with ExitStack() as ctx:
            layer1(nc, ctx, x, adj, L0_gnn_W, L0_gnn_B, out, h2, adj_slot, ident)
        with ExitStack() as ctx:
            layer2(nc, ctx, adj, L1_gnn_gcn_w, L1_gnn_gcn_b, L1_gnn_ln_g, L1_gnn_ln_b, L1_gnn_w_in, L1_gnn_conv_w,
                   L1_gnn_conv_b, L1_gnn_w_xp, L1_gnn_w_dt, L1_gnn_b_dt, L1_gnn_A_log, L1_gnn_D_skip, L1_gnn_w_out,
                   out, h2, adj_slot, ident)


_INS = ['x', 'adj', 'L0_gnn_W', 'L0_gnn_B', 'L1_gnn_gcn_w', 'L1_gnn_gcn_b', 'L1_gnn_ln_g', 'L1_gnn_ln_b',
        'L1_gnn_w_in', 'L1_gnn_conv_w', 'L1_gnn_conv_b', 'L1_gnn_w_xp', 'L1_gnn_w_dt', 'L1_gnn_b_dt',
        'L1_gnn_A_log', 'L1_gnn_D_skip', 'L1_gnn_w_out']


def kernel(**inputs):
    import numpy as _np
    import concourse.bacc as _bacc
    from concourse import mybir as _mybir
    from concourse.bass_utils import run_bass_kernel_spmd as _run

    nc = _bacc.Bacc("TRN2", target_bir_lowering=False, num_devices=1)
    arrays, args = {}, []
    for name in _INS:
        a = _np.ascontiguousarray(inputs[name])
        arrays[f"in_{name}_dram"] = a
        args.append(nc.dram_tensor(f"in_{name}_dram", a.shape, _mybir.dt.from_np(a.dtype), kind="ExternalInput").ap())
    out = nc.dram_tensor("out_0_dram", (N, D), _mybir.dt.float32, kind="ExternalOutput").ap()
    build(nc, *args, out)
    r = _run(nc, [arrays], core_ids=[0])
    return r.results[0]["out_0_dram"]
```

```python
from contextlib import ExitStack

import concourse.bass as bass
from concourse import mybir

F32 = mybir.dt.float32
BF16 = mybir.dt.bfloat16
ALU = mybir.AluOpType
ACT = mybir.ActivationFunctionType

P = 128
N = 8192
D = 128
RB = 4
GR = RB * P
G = N // GR
CW = 512
JB = CW // P
K = N // CW
SLOTS = 4
EDGES = 8
LAG = 4
DI = 256
H = DI // P
S = 16
RANK = 8
TAPS = 4
HIST = TAPS - 1
BC = 2 * S
EPS = 1e-5
TINY = 1e-12
ROWS_AT = 12
FINAL_AT = 8
PARAMS = 16
BANK = 512
LN_EXP = "natural_log_exp_and_others"


def after(eng, sem, count):
    if not isinstance(count, int) or count > 0:
        eng.wait_ge(sem, count)


class Chain:

    def __init__(self, eng, sem):
        self.eng, self.sem = eng, sem

    def __call__(self, instruction, count):
        instruction.then_inc(self.sem, 1)
        self.eng.wait_ge(self.sem, count)


def variance_steps(nc, stats, mean, var, diff):
    return [
        lambda: nc.vector.tensor_tensor(mean, stats[:, :, 1], stats[:, :, 4], ALU.add),
        lambda: nc.vector.tensor_tensor(diff, stats[:, :, 1], stats[:, :, 4], ALU.subtract),
        lambda: nc.vector.tensor_tensor(var, stats[:, :, 2], stats[:, :, 5], ALU.add),
        lambda: nc.vector.tensor_scalar(mean, mean, 0.5, None, ALU.mult),
        lambda: nc.vector.scalar_tensor_tensor(out=diff, in0=diff, scalar=0.25, in1=diff,
                                               op0=ALU.mult, op1=ALU.mult),
        lambda: nc.vector.scalar_tensor_tensor(out=var, in0=var, scalar=1.0 / D, in1=diff,
                                               op0=ALU.mult, op1=ALU.add),
        lambda: nc.vector.tensor_scalar(var, var, EPS, None, ALU.add),
    ]


VARIANCE = 7


def newton_steps(nc, root, var, work):
    return [
        lambda: nc.vector.tensor_tensor(work, root, root, ALU.mult),
        lambda: nc.vector.tensor_tensor(work, work, var, ALU.mult),
        lambda: nc.vector.tensor_scalar(work, work, -0.5, 1.5, ALU.mult, ALU.add),
        lambda: nc.vector.tensor_tensor(root, root, work, ALU.mult),
    ]


NEWTON = 4


def layer1(nc, ctx, x, adj, w0, b0, out, h2, adj_slot, ident):
    adj_v = adj.rearrange("(g r p) c -> g p r c", r=RB, p=P)
    x_v = x.rearrange("(g r p) d -> g p r d", r=RB, p=P)
    out_v = out.rearrange("(g r p) d -> g p r d", r=RB, p=P)
    x_all = x.rearrange("(b p) d -> p b d", p=P)

    def sb(name, shape, dt=F32):
        return ctx.enter_context(nc.sbuf_tensor(name, shape, dt))

    def sem(name):
        return ctx.enter_context(nc.semaphore(name))

    msg = sb("msg", [P, N // P, D])
    edge = sb("edge", [P, EDGES, JB * GR])
    w0_sb = sb("w0_sb", [D, D])
    b0_bc = sb("b0_bc", [P, RB, D])
    ht = sb("ht", [D, GR])
    yt = sb("yt", [D, GR])
    x_in = sb("x_in", [P, RB, D])
    x1 = sb("x1", [P, RB, D])
    stats0 = sb("stats0", [P, N // P, 6])
    mean0 = sb("mean0", [P, N // P])
    var0 = sb("var0", [P, N // P])
    root0 = sb("root0", [P, N // P])
    work0 = sb("work0", [P, N // P])
    stats = sb("stats", [P, RB, 6])
    mean = sb("mean", [P, RB])
    var = sb("var", [P, RB])
    root = sb("root", [P, RB])
    work = sb("work", [P, RB])
    ps = ctx.enter_context(nc.psum_tensor("ps_layer1", [P, 8 * BANK], F32))
    turn_ps = ps[:, 0:4 * BANK].rearrange("p (s c) -> p s c", s=2)
    acc = ps[:, 4 * BANK:5 * BANK]
    misc = ps[:, 5 * BANK:6 * BANK]
    turned_rows = ps[:, 6 * BANK:7 * BANK]
    messages = ps[:, 7 * BANK:8 * BANK]

    consts = sem("consts")
    weights = sem("weights")
    x_here = [sem(f"x_here{q}") for q in range(4)]
    stats_done = sem("stats_done")
    var_ready = sem("var_ready")
    ln_ready = sem("ln_ready")
    root_ready = sem("root_ready")
    normed = sem("normed")
    h_turned = sem("h_turned")
    ht_ready = sem("ht_ready")
    msg_ps = sem("msg_ps")
    msg_ready = sem("msg_ready")
    adj_here = [sem(f"adj_here{i}") for i in range(SLOTS)]
    masked = sem("masked")
    turned = sem("turned")
    ln_done = sem("ln_done")
    recip_done = sem("recip_done")
    expo_done = sem("expo_done")
    edge_ready = sem("edge_ready")
    mm_done = sem("mm_done")
    yt_ready = sem("yt_ready")
    y_turned = sem("y_turned")
    xg_here = sem("xg_here")
    x1_ready = sem("x1_ready")
    x1_kept = sem("x1_kept")
    v_own = sem("v_own")
    gvar_ready = sem("gvar_ready")
    gln_ready = sem("gln_ready")
    groot_ready = sem("groot_ready")
    h2_ready = sem("h2_ready")

    own = VARIANCE + NEWTON + 2

    with nc.Block() as block:
        @block.sync
        def _(sp):
            sp.dma_start(w0_sb[:, :], w0).then_inc(weights, 16)
            sp.dma_start(b0_bc[:, :, :], b0.rearrange("(o r d) -> o r d", o=1, r=1).to_broadcast([P, RB, D])
                         ).then_inc(weights, 16)
            for q in range(4):
                n = N // P // 4
                sp.dma_start(h2[:, q * n:(q + 1) * n, :], x_all[:, q * n:(q + 1) * n, :]
                             ).then_inc(x_here[q], 16)

            def load(g, k):
                after(sp, turned, 2 * (K * g + k) - 2 * SLOTS + 2)
                sp.dma_start(adj_slot[:, k % SLOTS], adj_v[g, :, :, k * CW:(k + 1) * CW]
                             ).then_inc(adj_here[k % SLOTS], 16)

            def fetch_rows(g):
                after(sp, x1_ready, g)
                sp.dma_start(x_in[:, :, :], x_v[g]).then_inc(xg_here, 16)

            def keep_rows(g):
                sp.wait_ge(x1_ready, g + 1)
                sp.dma_start(out_v[g], x1[:, :, :]).then_inc(x1_kept, 16)

            sp.sem_inc(x1_kept, 16)
            for k in range(K):
                load(0, k)
            fetch_rows(0)
            with sp.Fori(1, G) as g:
                for k in range(K):
                    load(g, k)
                    if k == ROWS_AT:
                        keep_rows(g - 1)
                        fetch_rows(g)
            keep_rows(G - 1)
            sp.wait_ge(x1_kept, 16 * (G + 1))

        @block.gpsimd
        def _(pool):
            nc.gpsimd.memset(ident[:, :], 0.0).then_inc(consts, 1)
            pool.wait_ge(consts, 1)
            nc.gpsimd.affine_select(out=ident[:, :], in_=ident[:, :], compare_op=ALU.not_equal, fill=1.0,
                                    base=0, pattern=[[-1, P]], channel_multiplier=1).then_inc(consts, 1)

        @block.scalar
        def _(act):
            nc.scalar.preload_act_table_set(LN_EXP)
            act.wait_ge(var_ready, 1)
            nc.scalar.activation(root0[:, :], var0[:, :], ACT.Ln).then_inc(ln_ready, 1)
            act.wait_ge(ln_ready, 1)
            nc.scalar.activation(root0[:, :], root0[:, :], ACT.Exp, scale=-0.5).then_inc(root_ready, 1)

            def relu_turned(i):
                act.wait_ge(h_turned, i + 1)
                after(act, msg_ps, i)
                nc.scalar.activation(ht[:, :], turned_rows, ACT.Relu).then_inc(ht_ready, 1)

            def weigh(g, k):
                act.wait_ge(expo_done, K * g + k + 1)
                e = edge[:, k % EDGES, :]
                nc.scalar.activation(e, e, ACT.Exp, scale=-2.0, bias=-2.0).then_inc(edge_ready, 1)

            def logarithm(g, k):
                c = K * g + k
                after(act, mm_done, c - EDGES + 1)
                for s in range(2):
                    act.wait_ge(turned, 2 * c + s + 1)
                    nc.scalar.activation(edge[:, k % EDGES, s * 2 * BANK:(s + 1) * 2 * BANK], turn_ps[:, s, :],
                                         ACT.Ln, bias=TINY).then_inc(ln_done, 1)

            def reciprocal(g, k):
                act.wait_ge(ln_done, 2 * (K * g + k) + 2)
                e = edge[:, k % EDGES, :]
                nc.scalar.activation(e, e, ACT.Exp, scale=-1.0).then_inc(recip_done, 1)

            def group_root(g):
                act.wait_ge(gvar_ready, g + 1)
                nc.scalar.activation(root[:, :], var[:, :], ACT.Ln).then_inc(gln_ready, 1)
                act.wait_ge(gln_ready, g + 1)
                nc.scalar.activation(root[:, :], root[:, :], ACT.Exp, scale=-0.5).then_inc(groot_ready, 1)

            for k in range(K):
                logarithm(0, k)
                if k >= 2:
                    weigh(0, k - 2)
                relu_turned(k)
                reciprocal(0, k)
            with act.Fori(1, G) as g:
                for k in range(K):
                    logarithm(g, k)
                    weigh(g, k - 2)
                    reciprocal(g, k)
                    if k == LAG + 4:
                        group_root(g - 1)
            weigh(G - 1, K - 2)
            weigh(G - 1, K - 1)
            group_root(G - 1)

        @block.vector
        def _(dve):
            chain = Chain(dve, v_own)
            for q in range(4):
                dve.wait_ge(x_here[q], 16)
                with dve.Fori(q * G // 4, (q + 1) * G // 4) as g:
                    for r in range(RB):
                        nc.vector.bn_stats(stats0[:, bass.ds(g * RB + r, 1), :], h2[:, bass.ds(g * RB + r, 1), :]
                                           ).then_inc(stats_done, 1)
            dve.wait_ge(stats_done, N // P)
            *most, last = variance_steps(nc, stats0, mean0[:, :], var0[:, :], work0[:, :])
            for n, step in enumerate(most):
                chain(step(), n + 1)
            last().then_inc(var_ready, 1)
            dve.wait_ge(var_ready, 1)
            dve.wait_ge(root_ready, 1)
            for n, step in enumerate(newton_steps(nc, root0[:, :], var0[:, :], work0[:, :])):
                chain(step(), VARIANCE + n)
            base0 = VARIANCE - 1 + NEWTON

            def norm_rows(i):
                for r in range(i * RB, (i + 1) * RB):
                    ins = nc.vector.tensor_scalar(h2[:, r, :], h2[:, r, :], mean0[:, r:r + 1], root0[:, r:r + 1],
                                                  ALU.subtract, ALU.mult)
                ins.then_inc(normed, 1)

            def add_bias(i):
                dve.wait_ge(msg_ps, i + 1)
                nc.vector.tensor_tensor(msg[:, i * RB:(i + 1) * RB, :],
                                        messages.rearrange("p (r d) -> p r d", r=RB),
                                        b0_bc[:, :, :], ALU.add).then_inc(msg_ready, 1)

            def mask(g, k):
                dve.wait_ge(adj_here[k % SLOTS], 16 * (K // SLOTS * g + k // SLOTS + 1))
                a = adj_slot[:, k % SLOTS]
                nc.vector.scalar_tensor_tensor(out=a, in0=a, scalar=1.0, in1=a, op0=ALU.is_lt, op1=ALU.mult
                                               ).then_inc(masked, 1)

            def exponent(g, k):
                dve.wait_ge(recip_done, K * g + k + 1)
                e = edge[:, k % EDGES, :]
                nc.vector.scalar_tensor_tensor(out=e, in0=e, scalar=2.0, in1=e, op0=ALU.subtract, op1=ALU.mult
                                               ).then_inc(expo_done, 1)

            def take_y(g):
                dve.wait_ge(mm_done, K * (g + 1))
                nc.vector.tensor_copy(yt[:, :], acc).then_inc(yt_ready, 1)

            def add_x(g):
                dve.wait_ge(y_turned, g + 1)
                dve.wait_ge(xg_here, 16 * (g + 1))
                dve.wait_ge(x1_kept, 16 * (g + 1))
                nc.vector.tensor_tensor(x1[:, :, :], misc.rearrange("p (r d) -> p r d", r=RB), x_in[:, :, :], ALU.add
                                        ).then_inc(x1_ready, 1)
                dve.wait_ge(x1_ready, g + 1)
                for r in range(RB):
                    ins = nc.vector.bn_stats(stats[:, r, :], x1[:, r, :])
                chain(ins, base0 + own * g + 1)

            def variance(g):
                o = base0 + own * g
                *most, last = variance_steps(nc, stats, mean[:, :], var[:, :], work[:, :])
                for n, step in enumerate(most):
                    chain(step(), o + 2 + n)
                last().then_inc(gvar_ready, 1)

            def newton(g):
                o = base0 + own * g + VARIANCE
                dve.wait_ge(groot_ready, g + 1)
                dve.wait_ge(gvar_ready, g + 1)
                for n, step in enumerate(newton_steps(nc, root[:, :], var[:, :], work[:, :])):
                    chain(step(), o + 1 + n)

            def norm_group(g):
                o = base0 + own * g + VARIANCE
                for r in range(RB):
                    ins = nc.vector.tensor_scalar(x_norm(g, r), x1[:, r, :], mean[:, r:r + 1], root[:, r:r + 1],
                                                  ALU.subtract, ALU.mult)
                chain(ins, o + 1 + NEWTON)
                blk = h2[:, bass.ds(RB * g, RB), :]
                chain(nc.vector.tensor_scalar(blk, blk, 0.0, None, ALU.max), o + 2 + NEWTON)

            def x_norm(g, r):
                return h2[:, bass.ds(RB * g + r, 1), :]

            dve.wait_ge(weights, 32)
            norm_rows(0)
            for k in range(K):
                if k + 1 < K:
                    norm_rows(k + 1)
                mask(0, k)
                if k >= 2:
                    exponent(0, k - 2)
                    add_bias(k - 2)
            add_bias(K - 2)
            add_bias(K - 1)
            with dve.Fori(1, G) as g:
                for k in range(K):
                    mask(g, k)
                    if k == LAG + 1:
                        take_y(g - 1)
                    exponent(g, k - 2)
                    if k == LAG + 3:
                        add_x(g - 1)
                    if k == LAG + 4:
                        variance(g - 1)
                    if k == LAG + 6:
                        newton(g - 1)
                    if k == LAG + 7:
                        norm_group(g - 1)
            exponent(G - 1, K - 2)
            exponent(G - 1, K - 1)
            take_y(G - 1)
            add_x(G - 1)
            variance(G - 1)
            newton(G - 1)
            norm_group(G - 1)

        @block.tensor
        def _(pe):
            pe.wait_ge(consts, 2)
            pe.wait_ge(weights, 32)

            def turn_rows(i):
                pe.wait_ge(normed, i + 1)
                after(pe, ht_ready, i)
                for r in range(RB):
                    ins = nc.tensor.transpose(turned_rows[:, r * P:(r + 1) * P], h2[:, i * RB + r, :], ident[:, :])
                ins.then_inc(h_turned, 1)

            def message(i):
                pe.wait_ge(ht_ready, i + 1)
                after(pe, msg_ready, i)
                for r in range(RB):
                    ins = nc.tensor.matmul(messages[:, r * D:(r + 1) * D], ht[:, r * P:(r + 1) * P], w0_sb[:, :],
                                           start=True, stop=True)
                ins.then_inc(msg_ps, 1)

            def turn(g, k):
                c = K * g + k
                pe.wait_ge(masked, c + 1)
                for s in range(2):
                    after(pe, ln_done, 2 * c + s - 1)
                    for b in range(2):
                        for r in range(RB):
                            ins = nc.tensor.transpose(turn_ps[:, s, b * GR + r * P:b * GR + (r + 1) * P],
                                                      adj_slot[:, k % SLOTS, r, (2 * s + b) * P:(2 * s + b + 1) * P],
                                                      ident[:, :])
                    ins.then_inc(turned, 1)

            def multiply(g, k):
                pe.wait_ge(edge_ready, K * g + k + 1)
                if k == 0:
                    after(pe, yt_ready, g)
                for b in range(JB):
                    j = k * JB + b
                    ins = nc.tensor.matmul(acc, msg[:, j, :], edge[:, k % EDGES, b * GR:(b + 1) * GR],
                                           start=(j == 0), stop=(j == N // P - 1))
                ins.then_inc(mm_done, 1)

            def turn_y(g):
                pe.wait_ge(yt_ready, g + 1)
                for r in range(RB):
                    ins = nc.tensor.transpose(misc[:, r * P:(r + 1) * P], yt[:, r * P:(r + 1) * P], ident[:, :])
                ins.then_inc(y_turned, 1)

            for k in range(K):
                turn_rows(k)
                turn(0, k)
                if k:
                    message(k - 1)
                if k >= LAG:
                    pe.wait_ge(msg_ready, k - LAG + 1)
                    multiply(0, k - LAG)
            message(K - 1)
            pe.wait_ge(msg_ready, K)
            with pe.Fori(1, G) as g:
                for k in range(K):
                    turn(g, k)
                    if k >= LAG:
                        multiply(g, k - LAG)
                    else:
                        multiply(g - 1, K + k - LAG)
                    if k == LAG + 1:
                        turn_y(g - 1)
            for k in range(K - LAG, K):
                multiply(G - 1, k)
            turn_y(G - 1)


def layer2(nc, ctx, adj, gcn_w, gcn_b, ln_g, ln_b, w_in, conv_w, conv_b, w_xp, w_dt, b_dt, a_log, d_skip, w_out,
           out, h2, adj_slot, ident):
    adj_v = adj.rearrange("(g r p) c -> g p r c", r=RB, p=P)
    out_v = out.rearrange("(g r p) d -> g p r d", r=RB, p=P)

    def sb(name, shape, dt=F32):
        return ctx.enter_context(nc.sbuf_tensor(name, shape, dt))

    def sem(name):
        return ctx.enter_context(nc.semaphore(name))

    gcn_w_sb = sb("gcn_w_sb", [D, D])
    gcn_b_row = sb("gcn_b_row", [1, D])
    ones_row = sb("ones_row", [1, P])
    ln_g_sb = sb("ln_g_sb", [D, 1])
    ln_b_sb = sb("ln_b_sb", [D, 1])
    w_in_sb = sb("w_in_sb", [D, 2 * DI])
    conv_w_sb = sb("conv_w_sb", [P, H, TAPS])
    conv_b_sb = sb("conv_b_sb", [P, H])
    w_xp_sb = sb("w_xp_sb", [P, H, 3 * BC + RANK])
    w_dt_sb = sb("w_dt_sb", [3 * BC + RANK, DI])
    b_dt_sb = sb("b_dt_sb", [P, H])
    a_sb = sb("a_sb", [P, H, S])
    d_sb = sb("d_sb", [P, H])
    w_out_sb = sb("w_out_sb", [P, H, D])
    one = sb("one", [P, 1])
    pick = sb("pick", [3 * BC, BC, P], BF16)

    turned_adj = sb("turned_adj", [P, 2, JB * GR])
    at = sb("at", [P, GR])
    hn = sb("hn", [P, RB, D])
    ht = sb("ht2", [D, GR])
    stats = sb("stats2", [P, RB, 6])
    mean = sb("mean2", [P, RB])
    var = sb("var2", [P, RB])
    root = sb("root2", [P, RB])
    work = sb("work2", [P, RB])
    xc = sb("xc", [P, H, HIST + GR])
    conv = sb("conv", [P, H, GR])
    zr = sb("zr", [P, H, GR])
    sig = sb("sig", [P, H, GR])
    u = sb("u", [P, H, GR])
    low = sb("low", [P, H, GR])
    rest = hn.rearrange("p r d -> p (r d)")
    dtr = at
    dt = sb("dt", [P, 2, H, GR])
    dtu = sb("dtu", [P, 2, H, GR])
    bcs = sb("bcs", [3 * BC, 2, GR], BF16)
    y = sb("y", [P, 2, H, GR])
    sz = sb("sz", [P, 2, H, GR])
    da = sb("da", [P, 2, H, GR])
    dbu = sb("dbu", [P, 2, H, GR])
    hs = sb("hs", [P, 2, H, GR])
    hc = sb("hc", [P, 2, H, GR])
    state = sb("state", [P, S, H])
    x1g = sb("x1g", [P, RB, D])
    og = sb("og", [P, RB, D])

    ps = ctx.enter_context(nc.psum_tensor("ps_layer2", [P, 8 * BANK], F32))

    def bank(n):
        return ps[:, n * BANK:(n + 1) * BANK]

    acc, misc = bank(2), bank(3)
    b_ps, c_ps = [bank(4), bank(5)], [bank(6), bank(7)]

    params = sem("params")
    consts = sem("consts2")
    a_exp = sem("a_exp")
    a_ready = sem("a_ready")
    adj_here = [sem(f"adj2_here{i}") for i in range(SLOTS)]
    turned = sem("turned2")
    kept = sem("kept2")
    mm_done = sem("mm2_done")
    at_ready = sem("at_ready")
    gcn_ps = sem("gcn_ps")
    gcn_relu = sem("gcn_relu")
    v_own = sem("v_own2")
    var_ready = sem("var2_ready")
    ln_ready = sem("ln2_ready")
    root_ready = sem("root2_ready")
    hn_ready = sem("hn_ready")
    hn_turned = sem("hn_turned")
    ht_ready = sem("ht2_ready")
    hist_ready = sem("hist_ready")
    xz_ps = sem("xz_ps")
    xz_ready = sem("xz_ready")
    conv_done = sem("conv_done")
    a_own = sem("a_own")
    sig_u = sem("sig_u")
    sig_z = sem("sig_z")
    u_ready = sem("u_ready")
    sz_ready = sem("sz_ready")
    y_start = sem("y_start")
    xp_ps = sem("xp_ps")
    xp_read = sem("xp_read")
    bcs_ready = sem("bcs_ready")
    dt_ps = sem("dt_ps")
    dt_arg = sem("dt_arg")
    soft_ready = sem("soft_ready")
    dt_ready = sem("dt_ready")
    dtu_ready = sem("dtu_ready")
    bc_ps = sem("bc_ps")
    da_ready = sem("da_ready")
    dbu_ready = sem("dbu_ready")
    scanned = sem("scanned")
    hc_ready = sem("hc_ready")
    y_added = sem("y_added")
    state_kept = sem("state_kept")
    y_gated = sem("y_gated")
    out_ps = sem("out_ps")
    og_ready = sem("og_ready")
    x1g_here = sem("x1g_here")
    og_kept = sem("og_kept")

    NORM, CONV, SPLIT, SOFT = 1 + VARIANCE - 1 + NEWTON, H * TAPS, 5, 3
    OWN = NORM + CONV + SPLIT + SOFT
    A_OWN = 6

    def walk(body, eng):
        for g in range(3):
            body(g, g % 2)
        with eng.Fori(3, G - 1, 2) as g:
            body(g, 1)
            body(g + 1, 0)
        for g in range(G - 1, G + 3):
            body(g, g % 2)

    def product_in(g):
        return not isinstance(g, int) or g < G

    def prep_in(g):
        return not isinstance(g, int) or 1 <= g <= G

    def items_in(g):
        return not isinstance(g, int) or 2 <= g <= G + 1

    def final_in(g):
        return not isinstance(g, int) or 3 <= g <= G + 2

    with nc.Block() as block:
        @block.sync
        def _(sp):
            def col(v):
                return v.rearrange("(h p) -> p h", p=P)

            b, dtc = w_xp[:, RANK:], w_xp[:, 0:RANK]
            loads = [
                (gcn_w_sb[:, :], gcn_w),
                (ln_g_sb[:, :], ln_g.rearrange("(p o) -> p o", o=1)),
                (ln_b_sb[:, :], ln_b.rearrange("(p o) -> p o", o=1)),
                (w_in_sb[:, :], w_in),
                (conv_w_sb[:, :, :], conv_w.rearrange("(h p) t -> p h t", p=P)),
                (w_dt_sb[3 * BC:3 * BC + RANK, :], w_dt),
                (a_sb[:, :, :], a_log.rearrange("(h p) s -> p h s", p=P)),
                (w_out_sb[:, :, :], w_out.rearrange("(h p) d -> p h d", p=P)),
                (w_xp_sb[:, :, 3 * BC:], dtc.rearrange("(h p) c -> p h c", p=P)),
            ]
            loads += [(w_xp_sb[:, :, q * BC:(q + 1) * BC], b.rearrange("(h p) c -> p h c", p=P)) for q in range(3)]
            loads += [(gcn_b_row[:, :], gcn_b.rearrange("(o d) -> o d", o=1))]
            assert len(loads) + 3 == PARAMS
            for dst, src in loads:
                sp.dma_start(dst, src).then_inc(params, 16)
            with nc.allow_non_contiguous_dma(reason="three short vectors, channels to partitions"):
                sp.dma_start(conv_b_sb[:, :], col(conv_b)).then_inc(params, 16)
                sp.dma_start(b_dt_sb[:, :], col(b_dt)).then_inc(params, 16)
                sp.dma_start(d_sb[:, :], col(d_skip)).then_inc(params, 16)

            def body(g, par):
                for k in range(K):
                    if product_in(g):
                        after(sp, turned, JB * (K * g + k - SLOTS + 1))
                        sp.dma_start(adj_slot[:, k % SLOTS], adj_v[g, :, :, k * CW:(k + 1) * CW]
                                     ).then_inc(adj_here[k % SLOTS], 16)
                    if k == ROWS_AT and final_in(g):
                        sp.wait_ge(og_ready, g - 2)
                        sp.dma_start(out_v[g - 3], og[:, :, :]).then_inc(og_kept, 16)
                    if k == ROWS_AT and final_in(g + 1):
                        after(sp, og_ready, g - 2)
                        sp.dma_start(x1g[:, :, :], out_v[g - 2]).then_inc(x1g_here, 16)

            sp.sem_inc(og_kept, 16)
            walk(body, sp)
            sp.wait_ge(og_kept, 16 * (G + 1))

        @block.gpsimd
        def _(pool):
            nc.gpsimd.memset(one[:, :], 1.0).then_inc(consts, 1)
            nc.gpsimd.memset(ones_row[:, :], 1.0).then_inc(consts, 1)
            nc.gpsimd.memset(state[:, :, :], 0.0).then_inc(consts, 1)
            nc.gpsimd.memset(xc[:, :, GR:], 0.0).then_inc(consts, 1)
            nc.gpsimd.memset(pick[:, :, :], 0.0).then_inc(consts, 1)
            pool.wait_ge(consts, 5)
            for q in range(3):
                nc.gpsimd.affine_select(out=pick[:, :, :], in_=pick[:, :, :], compare_op=ALU.not_equal, fill=1.0,
                                        base=-BC * q, pattern=[[-1, BC], [0, P]], channel_multiplier=1
                                        ).then_inc(consts, 1)
                pool.wait_ge(consts, 6 + q)

            def body(g, par):
                for k in range(K):
                    if k == 1 and prep_in(g):
                        after(pool, conv_done, H * (g - 1))
                        last = xc[:, :, GR:GR + HIST]
                        nc.gpsimd.tensor_tensor(xc[:, :, 0:HIST], last, ones3, ALU.mult).then_inc(hist_ready, 1)
                    if k == 0 and final_in(g):
                        v = y[:, 1 - par]
                        pool.wait_ge(y_added, K * (g - 2))
                        pool.wait_ge(sz_ready, g - 2)
                        nc.gpsimd.tensor_tensor(v, v, sz[:, 1 - par], ALU.mult).then_inc(y_gated, 1)
                    if items_in(g):
                        m = K * (g - 2) + k
                        v = y[:, par]
                        pool.wait_ge(hc_ready, m + 1)
                        if k:
                            pool.wait_ge(y_added, m)
                        else:
                            pool.wait_ge(y_start, H * (g - 1))
                        nc.gpsimd.tensor_tensor(v, v, hc[:, k % 2], ALU.add).then_inc(y_added, 1)
                        nc.gpsimd.tensor_copy(state[:, k, :], hs[:, k % 2, :, GR - 1]).then_inc(state_kept, 1)
                    if k == 12 and prep_in(g):
                        pool.wait_ge(u_ready, g)
                        after(pool, out_ps, g - 2)
                        for h in range(H):
                            nc.gpsimd.tensor_tensor(y[:, 1 - par, h, :], u[:, h, :],
                                                    d_sb[:, h:h + 1].to_broadcast([P, GR]), ALU.mult
                                                    ).then_inc(y_start, 1)

            ones3 = one[:, 0:1].rearrange("p (a b) -> p a b", a=1).to_broadcast([P, H, HIST])
            pool.wait_ge(params, 16 * PARAMS)
            walk(body, pool)

        @block.scalar
        def _(act):
            nc.scalar.preload_act_table_set(LN_EXP)
            act.wait_ge(params, 16 * PARAMS)
            act.wait_ge(consts, 8)
            nc.scalar.activation(a_sb[:, :, :], a_sb[:, :, :], ACT.Exp).then_inc(a_exp, 1)
            act.wait_ge(a_ready, 1)

            def sigmoid(src, n, g, done):
                o = A_OWN * (g - 1) + n
                nc.scalar.activation(sig[:, :, :], src, ACT.Exp, scale=-1.0).then_inc(a_own, 1)
                act.wait_ge(a_own, o + 1)
                nc.scalar.activation(sig[:, :, :], sig[:, :, :], ACT.Ln, bias=1.0).then_inc(a_own, 1)
                act.wait_ge(a_own, o + 2)
                nc.scalar.activation(sig[:, :, :], sig[:, :, :], ACT.Exp, scale=-1.0).then_inc(done, 1)

            def prep_first(g, par, k):
                if k == 1:
                    act.wait_ge(mm_done, K * g)
                    after(act, dt_ps, H * (g - 1))
                    nc.scalar.activation(at[:, :], acc, ACT.Identity).then_inc(at_ready, 1)
                if k == 2:
                    act.wait_ge(gcn_ps, g)
                    after(act, bcs_ready, g - 1)
                    nc.scalar.activation(hn[:, :, :], misc.rearrange("p (r d) -> p r d", r=RB), ACT.Relu
                                         ).then_inc(gcn_relu, 1)
                if k == 3:
                    act.wait_ge(hn_turned, g)
                    after(act, xz_ps, 4 * (g - 1))
                    nc.scalar.activation(ht[:, :], misc, ACT.Identity, scale=ln_g_sb[:, 0:1], bias=ln_b_sb[:, 0:1]
                                         ).then_inc(ht_ready, 1)
                if k in (4, 5, 6, 7):
                    q = k - 4
                    act.wait_ge(xz_ps, 4 * (g - 1) + q + 1)
                    if q == 0:
                        act.wait_ge(hist_ready, g)
                    if q == 2:
                        after(act, dt_ready, g - 1)
                    dst = xc[:, q, HIST:] if q < H else zr[:, q - H, :]
                    nc.scalar.activation(dst, misc, ACT.Identity).then_inc(xz_ready, 1)
                if k in (11, 12):
                    h = k - 11
                    act.wait_ge(dt_ps, H * (g - 1) + h + 1)
                    nc.scalar.activation(conv[:, h, :], misc, ACT.Identity, bias=b_dt_sb[:, h:h + 1]
                                         ).then_inc(dt_arg, 1)

            def prep_last(g, par, k):
                if k == 2:
                    act.wait_ge(var_ready, g)
                    nc.scalar.activation(root[:, :], var[:, :], ACT.Ln).then_inc(ln_ready, 1)
                    act.wait_ge(ln_ready, g)
                    nc.scalar.activation(root[:, :], root[:, :], ACT.Exp, scale=-0.5).then_inc(root_ready, 1)
                if k == 6:
                    act.wait_ge(conv_done, H * g)
                    after(act, dt_ready, g - 1)
                    sigmoid(conv[:, :, :], 0, g, sig_u)
                if k == 7:
                    act.wait_ge(u_ready, g)
                    act.wait_ge(xz_ready, 4 * g)
                    sigmoid(zr[:, :, :], 2, g, sig_z)
                if k == 12:
                    o = A_OWN * (g - 1) + 4
                    act.wait_ge(dt_arg, H * g)
                    act.wait_ge(sz_ready, g)
                    nc.scalar.activation(sig[:, :, :], conv[:, :, :], ACT.Abs).then_inc(a_own, 1)
                    act.wait_ge(a_own, o + 1)
                    nc.scalar.activation(sig[:, :, :], sig[:, :, :], ACT.Exp, scale=-1.0).then_inc(a_own, 1)
                    act.wait_ge(a_own, o + 2)
                    nc.scalar.activation(zr[:, :, :], sig[:, :, :], ACT.Ln, bias=1.0).then_inc(soft_ready, 1)

            def body(g, par):
                for k in range(K):
                    if prep_in(g):
                        prep_first(g, par, k)
                    if product_in(g):
                        after(act, mm_done, K * g + k - 1)
                        for b in range(JB):
                            act.wait_ge(turned, JB * (K * g + k) + b + 1)
                            nc.scalar.activation(turned_adj[:, k % 2, b * GR:(b + 1) * GR], bank(b % 2), ACT.Identity
                                                 ).then_inc(kept, 1)
                    if items_in(g):
                        m = K * (g - 2) + k
                        after(act, scanned, H * (m - 1))
                        if k == 0:
                            act.wait_ge(dt_ready, g - 1)
                        for h in range(H):
                            nc.scalar.activation(da[:, k % 2, h, :], dt[:, par, h, :], ACT.Exp,
                                                 scale=a_sb[:, h, k:k + 1]).then_inc(da_ready, 1)
                    if prep_in(g):
                        prep_last(g, par, k)

            walk(body, act)

        @block.vector
        def _(dve):
            chain = Chain(dve, v_own)
            dve.wait_ge(params, 16 * PARAMS)
            dve.wait_ge(consts, 8)
            dve.wait_ge(a_exp, 1)
            nc.vector.tensor_scalar(a_sb[:, :, :], a_sb[:, :, :], -1.0, None, ALU.mult).then_inc(a_ready, 1)

            def prep(g, par, k, last):
                o = OWN * (g - 1)
                if (k, last) == (2, False):
                    dve.wait_ge(gcn_relu, g)
                    for r in range(RB):
                        ins = nc.vector.bn_stats(stats[:, r, :], hn[:, r, :])
                    chain(ins, o + 1)
                    *most, final_step = variance_steps(nc, stats, mean[:, :], var[:, :], work[:, :])
                    for n, step in enumerate(most):
                        chain(step(), o + 2 + n)
                    final_step().then_inc(var_ready, 1)
                if (k, last) == (2, True):
                    dve.wait_ge(var_ready, g)
                    dve.wait_ge(root_ready, g)
                    for n, step in enumerate(newton_steps(nc, root[:, :], var[:, :], work[:, :])):
                        chain(step(), o + VARIANCE + 1 + n)
                    for r in range(RB):
                        ins = nc.vector.tensor_scalar(hn[:, r, :], hn[:, r, :], mean[:, r:r + 1], root[:, r:r + 1],
                                                      ALU.subtract, ALU.mult)
                    ins.then_inc(hn_ready, 1)
                o += NORM
                if k in (5, 6) and not last:
                    h = k - 5
                    dve.wait_ge(xz_ready, 4 * (g - 1) + h + 1)
                    dve.wait_ge(hist_ready, g)
                    after(dve, dt_ready, g - 1)
                    nc_first = nc.vector.tensor_scalar(conv[:, h, :], xc[:, h, 0:GR], conv_w_sb[:, h, 0:1],
                                                       conv_b_sb[:, h:h + 1], ALU.mult, ALU.add)
                    chain(nc_first, o + TAPS * h + 1)
                    for t in range(1, TAPS):
                        ins = nc.vector.scalar_tensor_tensor(out=conv[:, h, :], in0=xc[:, h, t:t + GR],
                                                             scalar=conv_w_sb[:, h, t:t + 1], in1=conv[:, h, :],
                                                             op0=ALU.mult, op1=ALU.add)
                        if t < TAPS - 1:
                            chain(ins, o + TAPS * h + 1 + t)
                        else:
                            ins.then_inc(conv_done, 1)
                            dve.wait_ge(conv_done, H * (g - 1) + h + 1)
                            dve.sem_inc(v_own, 1)
                o += CONV
                if (k, last) == (7, False):
                    dve.wait_ge(sig_u, g)
                    after(dve, dtu_ready, g - 1)
                    after(dve, y_start, H * (g - 1))
                    nc.vector.tensor_tensor(u[:, :, :], conv[:, :, :], sig[:, :, :], ALU.mult).then_inc(u_ready, 1)
                if (k, last) == (8, True):
                    dve.wait_ge(sig_z, g)
                    after(dve, y_gated, g - 2)
                    nc.vector.tensor_tensor(sz[:, 1 - par], zr[:, :, :], sig[:, :, :], ALU.mult).then_inc(sz_ready, 1)
                if (k, last) == (9, False):
                    full, parts = misc[0:3 * BC, :], bcs[:, 1 - par, :]
                    dve.wait_ge(xp_ps, g)
                    after(dve, bc_ps, K * (g - 2))
                    nc.vector.tensor_copy(dtr[3 * BC:3 * BC + RANK, :], misc[3 * BC:3 * BC + RANK, :]
                                          ).then_inc(xp_read, 1)
                    chain(nc.vector.tensor_copy(parts, full), o + 1)
                    nc.vector.tensor_tensor(rest[0:3 * BC, :], full, parts, ALU.subtract).then_inc(xp_read, 1)
                    dve.wait_ge(xp_read, 2 * g)
                    chain(nc.vector.tensor_copy(parts[BC:2 * BC, :], rest[BC:2 * BC, :]), o + 2)
                    chain(nc.vector.tensor_copy(parts[2 * BC:, :], rest[2 * BC:3 * BC, :]), o + 3)
                    chain(nc.vector.tensor_tensor(rest[2 * BC:3 * BC, :], rest[2 * BC:3 * BC, :], parts[2 * BC:, :],
                                                  ALU.subtract), o + 4)
                    chain(nc.vector.tensor_copy(parts[2 * BC:, :], rest[2 * BC:3 * BC, :]), o + 5)
                    dve.sem_inc(bcs_ready, 1)
                o += SPLIT
                if (k, last) == (13, False):
                    dve.wait_ge(soft_ready, g)
                    chain(nc.vector.tensor_scalar(low[:, :, :], sig[:, :, :], 1.0, 1.0, ALU.add, ALU.subtract), o + 1)
                    chain(nc.vector.tensor_tensor(low[:, :, :], sig[:, :, :], low[:, :, :], ALU.subtract), o + 2)
                    chain(nc.vector.tensor_tensor(low[:, :, :], low[:, :, :], zr[:, :, :], ALU.add), o + 3)
                    after(dve, da_ready, H * K * (g - 2))
                    nc.vector.scalar_tensor_tensor(out=dt[:, 1 - par], in0=conv[:, :, :], scalar=0.0,
                                                   in1=low[:, :, :], op0=ALU.max, op1=ALU.add).then_inc(dt_ready, 1)
                    dve.wait_ge(dt_ready, g)
                    after(dve, dbu_ready, K * (g - 2))
                    nc.vector.tensor_tensor(dtu[:, 1 - par], dt[:, 1 - par], u[:, :, :], ALU.mult
                                            ).then_inc(dtu_ready, 1)

            def item(g, par, k):
                m = K * (g - 2) + k
                b = k % 2
                dve.wait_ge(bc_ps, m + 1)
                dve.wait_ge(dtu_ready, g - 1)
                after(dve, scanned, H * (m - 1))
                nc.vector.tensor_tensor(dbu[:, b], dtu[:, par],
                                        b_ps[b].rearrange("p (o t) -> p o t", o=1).to_broadcast([P, H, GR]), ALU.mult
                                        ).then_inc(dbu_ready, 1)
                dve.wait_ge(dbu_ready, m + 1)
                dve.wait_ge(da_ready, H * (m + 1))
                if k == 0:
                    after(dve, state_kept, K * (g - 2))
                after(dve, state_kept, m - 1)
                after(dve, hc_ready, m - 1)
                for h in range(H):
                    nc.vector.tensor_tensor_scan(hs[:, b, h, :], da[:, b, h, :], dbu[:, b, h, :],
                                                 state[:, k, h:h + 1], ALU.mult, ALU.add).then_inc(scanned, 1)
                dve.wait_ge(scanned, H * (m + 1))
                after(dve, y_added, m - 1)
                nc.vector.tensor_tensor(hc[:, b], hs[:, b],
                                        c_ps[b].rearrange("p (o t) -> p o t", o=1).to_broadcast([P, H, GR]), ALU.mult
                                        ).then_inc(hc_ready, 1)

            def body(g, par):
                for k in range(K):
                    if k == FINAL_AT and final_in(g):
                        dve.wait_ge(out_ps, g - 2)
                        dve.wait_ge(x1g_here, 16 * (g - 2))
                        dve.wait_ge(og_kept, 16 * (g - 2))
                        nc.vector.tensor_tensor(og[:, :, :], misc.rearrange("p (r d) -> p r d", r=RB), x1g[:, :, :],
                                                ALU.add).then_inc(og_ready, 1)
                    if prep_in(g):
                        prep(g, par, k, False)
                    if items_in(g):
                        item(g, par, k)
                    if prep_in(g):
                        prep(g, par, k, True)

            walk(body, dve)

        @block.tensor
        def _(pe):
            pe.wait_ge(params, 16 * PARAMS)
            pe.wait_ge(consts, 8)

            def turn(g, k, b):
                n = JB * (K * g + k) + b
                if b == 0:
                    pe.wait_ge(adj_here[k % SLOTS], 16 * (K // SLOTS * g + k // SLOTS + 1))
                after(pe, kept, n - 1)
                for r in range(RB):
                    ins = nc.tensor.transpose(bank(b % 2)[:, r * P:(r + 1) * P],
                                              adj_slot[:, k % SLOTS, r, b * P:(b + 1) * P], ident[:, :])
                ins.then_inc(turned, 1)

            def multiply(g, k, b):
                j = k * JB + b
                pe.wait_ge(kept, JB * (K * g + k) + b + 1)
                if j == 0:
                    after(pe, at_ready, g)
                ins = nc.tensor.matmul(acc, h2[:, j, :], turned_adj[:, k % 2, b * GR:(b + 1) * GR],
                                       start=(j == 0), stop=(j == N // P - 1))
                if b == JB - 1:
                    ins.then_inc(mm_done, 1)

            def prep(g, par, k):
                if k == 2:
                    pe.wait_ge(at_ready, g)
                    after(pe, dt_arg, H * (g - 1))
                    for r in range(RB):
                        part = misc[:, r * D:(r + 1) * D]
                        nc.tensor.matmul(part, ones_row[:, :], gcn_b_row[:, :], start=True, stop=False)
                        ins = nc.tensor.matmul(part, at[:, r * P:(r + 1) * P], gcn_w_sb[:, :],
                                               start=False, stop=True)
                    ins.then_inc(gcn_ps, 1)
                if k == 3:
                    pe.wait_ge(hn_ready, g)
                    pe.wait_ge(gcn_relu, g)
                    for r in range(RB):
                        ins = nc.tensor.transpose(misc[:, r * P:(r + 1) * P], hn[:, r, :], ident[:, :])
                    ins.then_inc(hn_turned, 1)
                if k in (4, 5, 6, 7):
                    q = k - 4
                    pe.wait_ge(ht_ready, g)
                    if q:
                        pe.wait_ge(xz_ready, 4 * (g - 1) + q)
                    nc.tensor.matmul(misc, w_in_sb[:, q * P:(q + 1) * P], ht[:, :], start=True, stop=True
                                     ).then_inc(xz_ps, 1)
                if k == 9:
                    pe.wait_ge(u_ready, g)
                    if final_in(g):
                        pe.wait_ge(og_ready, g - 2)
                    for h in range(H):
                        ins = nc.tensor.matmul(misc[0:3 * BC + RANK, :], w_xp_sb[:, h, :], u[:, h, :],
                                               start=(h == 0), stop=(h == H - 1))
                    ins.then_inc(xp_ps, 1)
                if k in (11, 12):
                    h = k - 11
                    pe.wait_ge(xp_read, 2 * g)
                    if h:
                        pe.wait_ge(dt_arg, H * (g - 1) + h)
                    nc.tensor.matmul(misc, w_dt_sb[3 * BC:3 * BC + RANK, h * P:(h + 1) * P],
                                     dtr[3 * BC:3 * BC + RANK, :], start=True, stop=True).then_inc(dt_ps, 1)

            def spread(g, par, k):
                m = K * (g - 2) + k
                if k == 0:
                    pe.wait_ge(bcs_ready, g - 1)
                after(pe, hc_ready, m - 1)
                nc.tensor.matmul(b_ps[k % 2], pick[:, k, :], bcs[:, par, :], start=True, stop=True)
                nc.tensor.matmul(c_ps[k % 2], pick[:, S + k, :], bcs[:, par, :], start=True, stop=True
                                 ).then_inc(bc_ps, 1)

            def body(g, par):
                for k in range(K):
                    if prep_in(g):
                        prep(g, par, k)
                    if items_in(g):
                        spread(g, par, k)
                    for b in range(JB):
                        if product_in(g):
                            turn(g, k, b)
                        if b % 2:
                            for q in (b - 1, b):
                                if k and product_in(g):
                                    multiply(g, k - 1, q)
                                if k == 0 and prep_in(g):
                                    multiply(g - 1, K - 1, q)
                    if k == FINAL_AT and final_in(g):
                        v = y[:, 1 - par]
                        pe.wait_ge(y_gated, g - 2)
                        if prep_in(g):
                            pe.wait_ge(xz_ready, 4 * g)
                        else:
                            pe.wait_ge(dt_arg, H * G)
                            after(pe, og_ready, g - 3)
                        for r in range(RB):
                            for h in range(H):
                                ins = nc.tensor.matmul(misc[:, r * D:(r + 1) * D], v[:, h, r * P:(r + 1) * P],
                                                       w_out_sb[:, h, :], start=(h == 0), stop=(h == H - 1))
                        ins.then_inc(out_ps, 1)

            walk(body, pe)


def build(nc, x, adj, L0_gnn_W, L0_gnn_B, L1_gnn_gcn_w, L1_gnn_gcn_b, L1_gnn_ln_g, L1_gnn_ln_b, L1_gnn_w_in,
          L1_gnn_conv_w, L1_gnn_conv_b, L1_gnn_w_xp, L1_gnn_w_dt, L1_gnn_b_dt, L1_gnn_A_log, L1_gnn_D_skip,
          L1_gnn_w_out, out):
    with ExitStack() as both:
        h2 = both.enter_context(nc.sbuf_tensor("h2", [P, N // P, D], F32))
        adj_slot = both.enter_context(nc.sbuf_tensor("adj_slot", [P, SLOTS, RB, CW], F32))
        ident = both.enter_context(nc.sbuf_tensor("ident", [P, P], F32))
        with ExitStack() as ctx:
            layer1(nc, ctx, x, adj, L0_gnn_W, L0_gnn_B, out, h2, adj_slot, ident)
        with ExitStack() as ctx:
            layer2(nc, ctx, adj, L1_gnn_gcn_w, L1_gnn_gcn_b, L1_gnn_ln_g, L1_gnn_ln_b, L1_gnn_w_in, L1_gnn_conv_w,
                   L1_gnn_conv_b, L1_gnn_w_xp, L1_gnn_w_dt, L1_gnn_b_dt, L1_gnn_A_log, L1_gnn_D_skip, L1_gnn_w_out,
                   out, h2, adj_slot, ident)


_INS = ['x', 'adj', 'L0_gnn_W', 'L0_gnn_B', 'L1_gnn_gcn_w', 'L1_gnn_gcn_b', 'L1_gnn_ln_g', 'L1_gnn_ln_b',
        'L1_gnn_w_in', 'L1_gnn_conv_w', 'L1_gnn_conv_b', 'L1_gnn_w_xp', 'L1_gnn_w_dt', 'L1_gnn_b_dt',
        'L1_gnn_A_log', 'L1_gnn_D_skip', 'L1_gnn_w_out']


def kernel(**inputs):
    import numpy as _np
    import concourse.bacc as _bacc
    from concourse import mybir as _mybir
    from concourse.bass_utils import run_bass_kernel_spmd as _run

    nc = _bacc.Bacc("TRN2", target_bir_lowering=False, num_devices=1)
    arrays, args = {}, []
    for name in _INS:
        a = _np.ascontiguousarray(inputs[name])
        arrays[f"in_{name}_dram"] = a
        args.append(nc.dram_tensor(f"in_{name}_dram", a.shape, _mybir.dt.from_np(a.dtype), kind="ExternalInput").ap())
    out = nc.dram_tensor("out_0_dram", (N, D), _mybir.dt.float32, kind="ExternalOutput").ap()
    build(nc, *args, out)
    r = _run(nc, [arrays], core_ids=[0])
    return r.results[0]["out_0_dram"]
```

```python
from contextlib import ExitStack

import concourse.bass as bass
from concourse import mybir

F32 = mybir.dt.float32
F32R = mybir.dt.float32r
BF16 = mybir.dt.bfloat16
ALU = mybir.AluOpType
ACT = mybir.ActivationFunctionType

P = 128
N = 8192
D = 128
RB = 4
GR = RB * P
G = N // GR
CW = 512
JB = CW // P
K = N // CW
PARTED = 2
SLOTS = 4
EDGES = 8
LAG = 7
DI = 256
H = DI // P
S = 16
RANK = 8
TAPS = 4
HIST = TAPS - 1
BC = 2 * S
EPS = 1e-5
TINY = 1e-12
MESSAGES_AT = 7
ROWS_AT = 12
FINAL_AT = 3
PARAMS = 16
BANK = 512
LN_EXP = "natural_log_exp_and_others"


def after(eng, sem, count):
    if not isinstance(count, int) or count > 0:
        eng.wait_ge(sem, count)


class Chain:

    def __init__(self, eng, sem):
        self.eng, self.sem = eng, sem

    def __call__(self, instruction, count):
        instruction.then_inc(self.sem, 1)
        self.eng.wait_ge(self.sem, count)


def variance_steps(nc, stats, mean, var, diff):
    return [
        lambda: nc.vector.tensor_tensor(mean, stats[:, :, 1], stats[:, :, 4], ALU.add),
        lambda: nc.vector.tensor_tensor(diff, stats[:, :, 1], stats[:, :, 4], ALU.subtract),
        lambda: nc.vector.tensor_tensor(var, stats[:, :, 2], stats[:, :, 5], ALU.add),
        lambda: nc.vector.tensor_scalar(mean, mean, 0.5, None, ALU.mult),
        lambda: nc.vector.scalar_tensor_tensor(out=diff, in0=diff, scalar=0.25, in1=diff,
                                               op0=ALU.mult, op1=ALU.mult),
        lambda: nc.vector.scalar_tensor_tensor(out=var, in0=var, scalar=1.0 / D, in1=diff,
                                               op0=ALU.mult, op1=ALU.add),
        lambda: nc.vector.tensor_scalar(var, var, EPS, None, ALU.add),
    ]


VARIANCE = 7


def newton_steps(nc, root, var, work):
    return [
        lambda: nc.vector.tensor_tensor(work, root, root, ALU.mult),
        lambda: nc.vector.tensor_tensor(work, work, var, ALU.mult),
        lambda: nc.vector.tensor_scalar(work, work, -0.5, 1.5, ALU.mult, ALU.add),
        lambda: nc.vector.tensor_tensor(root, root, work, ALU.mult),
    ]


NEWTON = 4


def layer1(nc, ctx, sem, x, adj, w0, b0, out, h2, h2_hi, h2_lo, adj_slot, ident, p, done):
    adj_v = adj.rearrange("(g r p) c -> g p r c", r=RB, p=P)
    x_v = x.rearrange("(g r p) d -> g p r d", r=RB, p=P)
    out_v = out.rearrange("(g r p) d -> g p r d", r=RB, p=P)
    x_all = x.rearrange("(b p) d -> p b d", p=P)

    def sb(name, shape, dt=F32):
        return ctx.enter_context(nc.sbuf_tensor(name, shape, dt))

    msg = sb("msg", [P, N // P, D])
    edge = sb("edge", [P, EDGES, JB * GR])
    w0_sb = sb("w0_sb", [D, D])
    b0_bc = sb("b0_bc", [P, 2 * RB, D])
    yt = sb("yt", [D, GR])
    rows = yt.rearrange("p (r d) -> p r d", r=RB)
    x_both = sb("x_both", [P, 2, RB, D])
    x_in, x1 = x_both[:, 0], x_both[:, 1]
    ht = x_both.rearrange("p s r d -> p (s r d)")
    stats0 = sb("stats0", [P, N // P, 6])
    mean0 = sb("mean0", [P, N // P])
    var0 = sb("var0", [P, N // P])
    root0 = sb("root0", [P, N // P])
    work0 = sb("work0", [P, N // P])
    stats = sb("stats", [P, RB, 6])
    mean = sb("mean", [P, RB])
    var = sb("var", [P, RB])
    root = sb("root", [P, RB])
    work = sb("work", [P, RB])
    ps = ctx.enter_context(nc.psum_tensor("ps_layer1", [P, 8 * BANK], F32))
    turn_ps = ps[:, 0:4 * BANK].rearrange("p (s c) -> p s c", s=2)
    acc = ps[:, 4 * BANK:5 * BANK]
    misc = ps[:, 5 * BANK:6 * BANK]
    turned_rows = messages = ps[:, 6 * BANK:8 * BANK]

    consts = sem("consts")
    weights = sem("weights")
    x_here = [sem(f"x_here{q}") for q in range(4)]
    stats_done = sem("stats_done")
    var_ready = sem("var_ready")
    ln_ready = sem("ln_ready")
    root_ready = sem("root_ready")
    mean_off = sem("mean_off")
    root0_ready = sem("root0_ready")
    normed = sem("normed")
    h_turned = sem("h_turned")
    ht_ready = sem("ht_ready")
    msg_ps = sem("msg_ps")
    msg_ready = sem("msg_ready")
    adj_here = [sem(f"adj_here{i}") for i in range(SLOTS)]
    masked = sem("masked")
    turned = done["turned"]
    ln_done = sem("ln_done")
    recip_done = sem("recip_done")
    expo_done = sem("expo_done")
    edge_ready = sem("edge_ready")
    mm_done = done["mm_done"]
    yt_ready = sem("yt_ready")
    y_turned = sem("y_turned")
    xg_here = sem("xg_here")
    x1_ready = done["x1_ready"]
    x1_kept = done["x1_kept"]
    v_own = sem("v_own")
    gvar_ready = sem("gvar_ready")
    gln_ready = sem("gln_ready")
    groot_ready = sem("groot_ready")
    h2_ready = done["h2_ready"]

    own = VARIANCE + NEWTON + 4

    def sync(sp):
        def load(g, k):
            after(sp, turned, 2 * (K * g + k) - 2 * SLOTS + 2)
            sp.dma_start(adj_slot[:, k % SLOTS], adj_v[g, :, :, k * CW:(k + 1) * CW]
                         ).then_inc(adj_here[k % SLOTS], 16)

        def fetch_rows(g):
            sp.wait_ge(x1_kept, 16 * (g + 1))
            sp.dma_start(x_in, x_v[g]).then_inc(xg_here, 16)

        def keep_rows(g):
            sp.wait_ge(x1_ready, g + 1)
            sp.dma_start(out_v[g], x1).then_inc(x1_kept, 16)

        sp.sem_inc(x1_kept, 16)
        for k in range(K):
            load(0, k)
            if k < 4:
                n = N // P // 4
                sp.dma_start(msg[:, k * n:(k + 1) * n, :], x_all[:, k * n:(k + 1) * n, :]
                             ).then_inc(x_here[k], 16)
            if k == 3:
                sp.dma_start(w0_sb[:, :], w0).then_inc(weights, 16)
                sp.dma_start(b0_bc[:, :, :], b0.rearrange("(o r d) -> o r d", o=1, r=1
                                                          ).to_broadcast([P, 2 * RB, D])).then_inc(weights, 16)
            if k == K // 2:
                p["load"](sp)
        sp.wait_ge(msg_ps, K // 2)
        with sp.Fori(1, G) as g:
            for k in range(K):
                load(g, k)
                if k == 2:
                    fetch_rows(g - 1)
                if k == ROWS_AT + 2:
                    keep_rows(g - 1)
        fetch_rows(G - 1)

    def keep_last_rows(sp):
        sp.wait_ge(x1_ready, G)
        sp.dma_start(out_v[G - 1], x1).then_inc(x1_kept, 16)

    def gpsimd(pool):
        nc.gpsimd.memset(ident[:, :], 0.0).then_inc(consts, 1)
        pool.wait_ge(consts, 1)
        nc.gpsimd.affine_select(out=ident[:, :], in_=ident[:, :], compare_op=ALU.not_equal, fill=1.0,
                                base=0, pattern=[[-1, P]], channel_multiplier=1).then_inc(consts, 1)

        p["make"](pool)
        pool.wait_ge(root0_ready, 1)
        for j in range(K // 2):
            rows_j = slice(2 * RB * j, 2 * RB * (j + 1))
            v = msg[:, rows_j, :]

            def wide(per_row):
                return per_row[:, rows_j].rearrange("p (r o) -> p r o", o=1).to_broadcast([P, 2 * RB, D])

            nc.gpsimd.tensor_tensor(v, v, wide(mean0), ALU.subtract).then_inc(mean_off, 1)
            pool.wait_ge(mean_off, j + 1)
            nc.gpsimd.tensor_tensor(v, v, wide(root0), ALU.mult).then_inc(normed, 1)

    def group_root(act, g):
        act.wait_ge(gvar_ready, g + 1)
        nc.scalar.activation(root[:, :], var[:, :], ACT.Ln).then_inc(gln_ready, 1)
        act.wait_ge(gln_ready, g + 1)
        nc.scalar.activation(root[:, :], root[:, :], ACT.Exp, scale=-0.5).then_inc(groot_ready, 1)

    def scalar(act):
        nc.scalar.preload_act_table_set(LN_EXP)

        def relu_turned(i):
            act.wait_ge(h_turned, i + 1)
            after(act, msg_ps, i)
            nc.scalar.activation(ht, turned_rows, ACT.Relu).then_inc(ht_ready, 1)

        def weigh(g, k):
            act.wait_ge(expo_done, K * g + k + 1)
            e = edge[:, k % EDGES, :]
            nc.scalar.activation(e, e, ACT.Exp, scale=-2.0, bias=-2.0).then_inc(edge_ready, 1)

        def logarithm(g, k):
            c = K * g + k
            after(act, mm_done, c - EDGES + 1)
            for s in range(2):
                act.wait_ge(turned, 2 * c + s + 1)
                nc.scalar.activation(edge[:, k % EDGES, s * 2 * BANK:(s + 1) * 2 * BANK], turn_ps[:, s, :],
                                     ACT.Ln, bias=TINY).then_inc(ln_done, 1)

        def reciprocal(g, k):
            act.wait_ge(ln_done, 2 * (K * g + k) + 2)
            e = edge[:, k % EDGES, :]
            nc.scalar.activation(e, e, ACT.Exp, scale=-1.0).then_inc(recip_done, 1)

        def rows_root():
            act.wait_ge(var_ready, 1)
            nc.scalar.activation(root0[:, :], var0[:, :], ACT.Ln).then_inc(ln_ready, 1)
            act.wait_ge(ln_ready, 1)
            nc.scalar.activation(root0[:, :], root0[:, :], ACT.Exp, scale=-0.5).then_inc(root_ready, 1)

        for k in range(K):
            if 0 <= k - MESSAGES_AT < K // 2:
                relu_turned(k - MESSAGES_AT)
            logarithm(0, k)
            if k >= 2:
                weigh(0, k - 2)
            reciprocal(0, k)
            if k == 4:
                rows_root()
        with act.Fori(1, G) as g:
            for k in range(K):
                logarithm(g, k)
                weigh(g, k - 2)
                reciprocal(g, k)
                if k == LAG + 4:
                    group_root(act, g - 1)
        weigh(G - 1, K - 2)
        weigh(G - 1, K - 1)

    def vector(dve):
        chain = Chain(dve, v_own)
        base0 = VARIANCE - 1 + NEWTON

        def rows_stats(q):
            n = N // P // 4
            dve.wait_ge(x_here[q], 16)
            for r in range(q * n, (q + 1) * n):
                ins = nc.vector.bn_stats(stats0[:, r, :], msg[:, r, :])
            ins.then_inc(stats_done, 1)

        def rows_variance():
            dve.wait_ge(stats_done, 4)
            *most, last = variance_steps(nc, stats0, mean0[:, :], var0[:, :], work0[:, :])
            for n, step in enumerate(most):
                chain(step(), n + 1)
            last().then_inc(var_ready, 1)

        def rows_newton():
            dve.wait_ge(var_ready, 1)
            dve.wait_ge(root_ready, 1)
            for n, step in enumerate(newton_steps(nc, root0[:, :], var0[:, :], work0[:, :])):
                chain(step(), VARIANCE + n)
            dve.sem_inc(root0_ready, 1)

        def add_bias(i):
            dve.wait_ge(msg_ps, i + 1)
            nc.vector.tensor_tensor(msg[:, 2 * i * RB:2 * (i + 1) * RB, :],
                                    messages.rearrange("p (r d) -> p r d", r=2 * RB),
                                    b0_bc[:, :, :], ALU.add).then_inc(msg_ready, 1)

        def mask(g, k):
            dve.wait_ge(adj_here[k % SLOTS], 16 * (K // SLOTS * g + k // SLOTS + 1))
            a = adj_slot[:, k % SLOTS]
            nc.vector.scalar_tensor_tensor(out=a, in0=a, scalar=1.0, in1=a, op0=ALU.is_lt, op1=ALU.mult
                                           ).then_inc(masked, 1)

        def exponent(g, k):
            dve.wait_ge(recip_done, K * g + k + 1)
            e = edge[:, k % EDGES, :]
            nc.vector.scalar_tensor_tensor(out=e, in0=e, scalar=2.0, in1=e, op0=ALU.subtract, op1=ALU.mult
                                           ).then_inc(expo_done, 1)

        def take_y(g):
            dve.wait_ge(mm_done, K * (g + 1))
            nc.vector.tensor_copy(yt[:, :], acc).then_inc(yt_ready, 1)

        def add_x(g):
            dve.wait_ge(y_turned, g + 1)
            dve.wait_ge(xg_here, 16 * (g + 1))
            dve.wait_ge(x1_kept, 16 * (g + 1))
            nc.vector.tensor_tensor(x1, misc.rearrange("p (r d) -> p r d", r=RB), x_in, ALU.add
                                    ).then_inc(x1_ready, 1)
            dve.wait_ge(x1_ready, g + 1)
            for r in range(RB):
                ins = nc.vector.bn_stats(stats[:, r, :], x1[:, r, :])
            chain(ins, base0 + own * g + 1)

        def variance(g):
            o = base0 + own * g
            *most, last = variance_steps(nc, stats, mean[:, :], var[:, :], work[:, :])
            for n, step in enumerate(most):
                chain(step(), o + 2 + n)
            last().then_inc(gvar_ready, 1)

        def newton(g):
            o = base0 + own * g + VARIANCE
            dve.wait_ge(groot_ready, g + 1)
            dve.wait_ge(gvar_ready, g + 1)
            for n, step in enumerate(newton_steps(nc, root[:, :], var[:, :], work[:, :])):
                chain(step(), o + 1 + n)

        def norm_group(g):
            o = base0 + own * g + VARIANCE
            for r in range(RB):
                ins = nc.vector.tensor_scalar(rows[:, r, :], x1[:, r, :], mean[:, r:r + 1], root[:, r:r + 1],
                                              ALU.subtract, ALU.mult)
            chain(ins, o + 1 + NEWTON)
            hi = h2_hi[:, bass.ds(PARTED * g, PARTED), :]
            lo = h2_lo[:, bass.ds(PARTED * g, PARTED), :]
            whole = h2[:, bass.ds((RB - PARTED) * g, RB - PARTED), :]
            nc.vector.tensor_scalar(whole, rows[:, PARTED:, :], 0.0, None, ALU.max)
            first = rows[:, 0:PARTED, :]
            chain(nc.vector.tensor_scalar(first, first, 0.0, None, ALU.max), o + 2 + NEWTON)
            chain(nc.vector.tensor_copy(hi, first), o + 3 + NEWTON)
            chain(nc.vector.tensor_tensor(lo, first, hi.bitcast(F32), ALU.subtract), o + 4 + NEWTON)
            dve.sem_inc(h2_ready, 1)

        for k in range(K):
            mask(0, k)
            if k >= 2:
                exponent(0, k - 2)
            if k < 4:
                rows_stats(k)
            if k == 4:
                rows_variance()
            if k == 5:
                rows_newton()
            if 0 <= k - MESSAGES_AT < K // 2:
                if k == MESSAGES_AT:
                    dve.wait_ge(weights, 32)
                add_bias(k - MESSAGES_AT)
        with dve.Fori(1, G) as g:
            for k in range(K):
                mask(g, k)
                if k == LAG + 1:
                    take_y(g - 1)
                exponent(g, k - 2)
                if k == LAG + 3:
                    add_x(g - 1)
                if k == LAG + 4:
                    variance(g - 1)
                if k == LAG + 6:
                    newton(g - 1)
                if k == LAG + 7:
                    norm_group(g - 1)
        exponent(G - 1, K - 2)
        exponent(G - 1, K - 1)
        take_y(G - 1)
        add_x(G - 1)
        variance(G - 1)
        newton(G - 1)
        norm_group(G - 1)

    def turn_y(pe, g):
        pe.wait_ge(yt_ready, g + 1)
        for r in range(RB):
            ins = nc.tensor.transpose(misc[:, r * P:(r + 1) * P], yt[:, r * P:(r + 1) * P], ident[:, :])
        ins.then_inc(y_turned, 1)

    def tensor(pe):
        pe.wait_ge(consts, 2)

        def turn_rows(i):
            pe.wait_ge(normed, i + 1)
            after(pe, msg_ready, i)
            for r in range(2 * RB):
                ins = nc.tensor.transpose(turned_rows[:, r * P:(r + 1) * P], msg[:, 2 * i * RB + r, :],
                                          ident[:, :])
            ins.then_inc(h_turned, 1)

        def message(i):
            pe.wait_ge(ht_ready, i + 1)
            for r in range(2 * RB):
                ins = nc.tensor.matmul(messages[:, r * D:(r + 1) * D], ht[:, r * P:(r + 1) * P], w0_sb[:, :],
                                       start=True, stop=True)
            ins.then_inc(msg_ps, 1)

        def turn(g, k):
            c = K * g + k
            pe.wait_ge(masked, c + 1)
            for s in range(2):
                after(pe, ln_done, 2 * c + s - 1)
                for b in range(2):
                    for r in range(RB):
                        ins = nc.tensor.transpose(turn_ps[:, s, b * GR + r * P:b * GR + (r + 1) * P],
                                                  adj_slot[:, k % SLOTS, r, (2 * s + b) * P:(2 * s + b + 1) * P],
                                                  ident[:, :])
                ins.then_inc(turned, 1)

        def multiply(g, k):
            pe.wait_ge(edge_ready, K * g + k + 1)
            if k == 0:
                after(pe, yt_ready, g)
            for b in range(JB):
                j = k * JB + b
                ins = nc.tensor.matmul(acc, msg[:, j, :], edge[:, k % EDGES, b * GR:(b + 1) * GR],
                                       start=(j == 0), stop=(j == N // P - 1))
            ins.then_inc(mm_done, 1)

        for k in range(K):
            turn(0, k)
            if 0 <= k - MESSAGES_AT < K // 2:
                if k == MESSAGES_AT:
                    pe.wait_ge(weights, 32)
                message(k - MESSAGES_AT)
            if k >= LAG:
                pe.wait_ge(msg_ready, (k - LAG) // 2 + 1)
                multiply(0, k - LAG)
            if 0 <= k + 1 - MESSAGES_AT < K // 2:
                turn_rows(k + 1 - MESSAGES_AT)
        pe.wait_ge(msg_ready, K // 2)
        with pe.Fori(1, G) as g:
            for k in range(K):
                turn(g, k)
                if k >= LAG:
                    multiply(g, k - LAG)
                else:
                    multiply(g - 1, K + k - LAG)
                if k == LAG + 1:
                    turn_y(pe, g - 1)
        for k in range(K - LAG, K):
            multiply(G - 1, k)

    last_steps = {"turn": lambda pe: turn_y(pe, G - 1), "root": lambda act: group_root(act, G - 1),
                  "keep": keep_last_rows}
    return (sync, gpsimd, scalar, vector, tensor), last_steps


def parameters(nc, both, sem, gcn_w, gcn_b, ln_g, ln_b, w_in, conv_w, conv_b, w_xp, w_dt, b_dt, a_log,
               d_skip, w_out):
    def sb(name, shape, dt=F32):
        return both.enter_context(nc.sbuf_tensor(name, shape, dt))

    gcn_w_sb = sb("gcn_w_sb", [D, D])
    gcn_b_row = sb("gcn_b_row", [1, D])
    ones_row = sb("ones_row", [1, P])
    ln_g_sb = sb("ln_g_sb", [D, 1])
    ln_b_sb = sb("ln_b_sb", [D, 1])
    w_in_sb = sb("w_in_sb", [D, 2 * DI])
    conv_w_sb = sb("conv_w_sb", [P, H, TAPS])
    conv_b_sb = sb("conv_b_sb", [P, H])
    w_xp_sb = sb("w_xp_sb", [P, H, 3 * BC + RANK])
    w_dt_sb = sb("w_dt_sb", [3 * BC + RANK, DI])
    b_dt_sb = sb("b_dt_sb", [P, H])
    a_sb = sb("a_sb", [P, H, S])
    d_sb = sb("d_sb", [P, H])
    w_out_sb = sb("w_out_sb", [P, H, D])
    one = sb("one", [P, 1])
    pick = sb("pick", [3 * BC, BC, P], BF16)
    params = sem("params")
    consts = sem("consts2")

    def load(sp):
        def col(v):
            return v.rearrange("(h p) -> p h", p=P)

        b, dtc = w_xp[:, RANK:], w_xp[:, 0:RANK]
        loads = [
            (gcn_w_sb[:, :], gcn_w),
            (ln_g_sb[:, :], ln_g.rearrange("(p o) -> p o", o=1)),
            (ln_b_sb[:, :], ln_b.rearrange("(p o) -> p o", o=1)),
            (w_in_sb[:, :], w_in),
            (conv_w_sb[:, :, :], conv_w.rearrange("(h p) t -> p h t", p=P)),
            (w_dt_sb[3 * BC:3 * BC + RANK, :], w_dt),
            (a_sb[:, :, :], a_log.rearrange("(h p) s -> p h s", p=P)),
            (w_out_sb[:, :, :], w_out.rearrange("(h p) d -> p h d", p=P)),
            (w_xp_sb[:, :, 3 * BC:], dtc.rearrange("(h p) c -> p h c", p=P)),
        ]
        loads += [(w_xp_sb[:, :, q * BC:(q + 1) * BC], b.rearrange("(h p) c -> p h c", p=P)) for q in range(3)]
        loads += [(gcn_b_row[:, :], gcn_b.rearrange("(o d) -> o d", o=1))]
        assert len(loads) + 3 == PARAMS
        for dst, src in loads:
            sp.dma_start(dst, src).then_inc(params, 16)
        with nc.allow_non_contiguous_dma(reason="three short vectors, channels to partitions"):
            sp.dma_start(conv_b_sb[:, :], col(conv_b)).then_inc(params, 16)
            sp.dma_start(b_dt_sb[:, :], col(b_dt)).then_inc(params, 16)
            sp.dma_start(d_sb[:, :], col(d_skip)).then_inc(params, 16)

    def make(pool):
        nc.gpsimd.memset(one[:, :], 1.0).then_inc(consts, 1)
        nc.gpsimd.memset(ones_row[:, :], 1.0).then_inc(consts, 1)
        nc.gpsimd.memset(pick[:, :, :], 0.0).then_inc(consts, 1)
        pool.wait_ge(consts, 3)
        for q in range(3):
            nc.gpsimd.affine_select(out=pick[:, :, :], in_=pick[:, :, :], compare_op=ALU.not_equal, fill=1.0,
                                    base=-BC * q, pattern=[[-1, BC], [0, P]], channel_multiplier=1
                                    ).then_inc(consts, 1)
            pool.wait_ge(consts, 4 + q)

    return {"gcn_w_sb": gcn_w_sb, "gcn_b_row": gcn_b_row, "ones_row": ones_row, "ln_g_sb": ln_g_sb,
            "ln_b_sb": ln_b_sb, "w_in_sb": w_in_sb, "conv_w_sb": conv_w_sb, "conv_b_sb": conv_b_sb,
            "w_xp_sb": w_xp_sb, "w_dt_sb": w_dt_sb, "b_dt_sb": b_dt_sb, "a_sb": a_sb, "d_sb": d_sb,
            "w_out_sb": w_out_sb, "one": one, "pick": pick, "params": params, "consts": consts, "load": load,
            "make": make}


def layer2(nc, ctx, sem, adj, p, out, h2, h2_hi, h2_lo, adj_slot, ident, done, last_steps):
    adj_v = adj.rearrange("(g r p) c -> g p r c", r=RB, p=P)
    out_v = out.rearrange("(g r p) d -> g p r d", r=RB, p=P)

    def sb(name, shape, dt=F32):
        return ctx.enter_context(nc.sbuf_tensor(name, shape, dt))

    gcn_w_sb = p["gcn_w_sb"]
    gcn_b_row = p["gcn_b_row"]
    ones_row = p["ones_row"]
    ln_g_sb = p["ln_g_sb"]
    ln_b_sb = p["ln_b_sb"]
    w_in_sb = p["w_in_sb"]
    conv_w_sb = p["conv_w_sb"]
    conv_b_sb = p["conv_b_sb"]
    w_xp_sb = p["w_xp_sb"]
    w_dt_sb = p["w_dt_sb"]
    b_dt_sb = p["b_dt_sb"]
    a_sb = p["a_sb"]
    d_sb = p["d_sb"]
    w_out_sb = p["w_out_sb"]
    one = p["one"]
    pick = p["pick"]
    params, consts = p["params"], p["consts"]

    ps = ctx.enter_context(nc.psum_tensor("ps_layer2", [P, 8 * BANK], F32))
    whole = sb("whole", [P, 2, JB - PARTED, GR])
    full = sb("full", [P, PARTED, GR])
    hi = sb("hi", [P, 2, PARTED, GR], F32R)
    lo = sb("lo", [P, 2, PARTED, GR], F32R)
    at = sb("at", [P, GR])
    hn = sb("hn", [P, RB, D])
    stats = sb("stats2", [P, RB, 6])
    mean = sb("mean2", [P, RB])
    var = sb("var2", [P, RB])
    root = sb("root2", [P, RB])
    work = sb("work2", [P, RB])
    xc = sb("xc", [P, H, HIST + GR])
    conv = sb("conv", [P, H, GR])
    zr = sb("zr", [P, H, GR])
    sig = sb("sig", [P, H, GR])
    u = sb("u", [P, H, GR])
    rest = hn.rearrange("p r d -> p (r d)")
    ht = dtr = at
    low = xc[:, :, 0:GR]
    dt = sb("dt", [P, 2, H, GR])
    dtu = sb("dtu", [P, 2, H, GR])
    bcs = sb("bcs", [3 * BC, 2, GR], BF16)
    y = sb("y", [P, 2, H, GR])
    sz = sb("sz", [P, 2, H, GR])
    da = sb("da", [P, 2, H, GR])
    dbu = sb("dbu", [P, 2, H, GR])
    hs = sb("hs", [P, 2, H, GR])
    hc = dbu
    tail_hc, tail_c = whole, full
    y_sum = ps[:, 0:2 * BANK].rearrange("p (h t) -> p h t", h=H)
    state = sb("state", [P, S, H])
    og = sb("og", [P, RB, D])


    def bank(n):
        return ps[:, n * BANK:(n + 1) * BANK]

    acc, misc = bank(2), bank(3)
    b_ps, c_ps = [bank(4), bank(5)], [bank(6), bank(7)]

    zeros = sem("zeros")
    a_exp = sem("a_exp")
    a_ready = sem("a_ready")
    adj_here = [sem(f"adj2_here{i}") for i in range(SLOTS)]
    turned = sem("turned2")
    kept = sem("kept2")
    lo_ready = sem("lo_ready")
    mm_done = sem("mm2_done")
    at_ready = sem("at_ready")
    gcn_ps = sem("gcn_ps")
    gcn_relu = sem("gcn_relu")
    v_own = sem("v_own2")
    var_ready = sem("var2_ready")
    ln_ready = sem("ln2_ready")
    root_ready = sem("root2_ready")
    hn_ready = sem("hn_ready")
    hn_turned = sem("hn_turned")
    ht_ready = sem("ht2_ready")
    hist_ready = sem("hist_ready")
    xz_ps = sem("xz_ps")
    xz_ready = sem("xz_ready")
    conv_done = sem("conv_done")
    a_own = sem("a_own")
    sig_u = sem("sig_u")
    sig_z = sem("sig_z")
    u_ready = sem("u_ready")
    sz_ready = sem("sz_ready")
    y_start = sem("y_start")
    xp_ps = sem("xp_ps")
    xp_read = sem("xp_read")
    bcs_ready = sem("bcs_ready")
    dt_ps = sem("dt_ps")
    dt_arg = sem("dt_arg")
    soft_ready = sem("soft_ready")
    dt_ready = sem("dt_ready")
    dtu_ready = sem("dtu_ready")
    bc_ps = sem("bc_ps")
    da_ready = sem("da_ready")
    dbu_ready = sem("dbu_ready")
    scanned = sem("scanned")
    hc_ready = sem("hc_ready")
    y_added = sem("y_added")
    state_kept = sem("state_kept")
    y_gated = sem("y_gated")
    y_summed = sem("y_summed")
    c_kept = sem("c_kept")
    out_ps = sem("out_ps")
    og_ready = sem("og_ready")
    x1g_here = sem("x1g_here")
    og_kept = sem("og_kept")

    NORM, CONV, PARTS, SOFT = 1 + VARIANCE - 1 + NEWTON, H * TAPS, 5, 3
    OWN = NORM + CONV + PARTS + SOFT
    A_OWN = 8

    def walk(body, eng):
        for g in range(3):
            body(g, g % 2)
        with eng.Fori(3, G - 1, 2) as g:
            body(g, 1)
            body(g + 1, 0)
        for g in range(G - 1, G + 3):
            body(g, g % 2)

    def product_in(g):
        return not isinstance(g, int) or g < G

    def prep_in(g):
        return not isinstance(g, int) or 1 <= g <= G

    def items_in(g):
        return not isinstance(g, int) or 2 <= g <= G + 1

    def tail(g):
        return isinstance(g, int) and g >= G

    def final_in(g):
        return not isinstance(g, int) or 3 <= g <= G + 2

    def sync(sp):
        def body(g, par):
            for k in range(K):
                if product_in(g):
                    if isinstance(g, int) and K * g + k < SLOTS:
                        sp.wait_ge(done["turned"], 2 * (K * G + k - SLOTS + 1))
                    else:
                        sp.wait_ge(turned, JB * (K * g + k - SLOTS + 1))
                    sp.dma_start(adj_slot[:, k % SLOTS], adj_v[g, :, :, k * CW:(k + 1) * CW]
                                 ).then_inc(adj_here[k % SLOTS], 16)
                if k == ROWS_AT and final_in(g):
                    sp.wait_ge(og_ready, g - 2)
                    sp.dma_start(out_v[g - 3], og[:, :, :]).then_inc(og_kept, 16)
                if isinstance(g, int) and (g, k) == (0, SLOTS):
                    last_steps["keep"](sp)
                if k == ROWS_AT + 2 and final_in(g + 1):
                    if isinstance(g, int) and g == 2:
                        sp.wait_ge(done["x1_kept"], 16 * (G + 1))
                    after(sp, og_kept, 16 * (g - 2))
                    sp.dma_start(og[:, :, :], out_v[g - 2]).then_inc(x1g_here, 16)

        walk(body, sp)
        sp.wait_ge(og_kept, 16 * G)

    def gpsimd(pool):
        def add_item(g, par, k):
            m = K * (g - 2) + k
            v = y[:, par]
            pool.wait_ge(hc_ready, m + 1)
            if k:
                pool.wait_ge(y_added, m)
            else:
                pool.wait_ge(y_start, H * (g - 1))
            nc.gpsimd.tensor_tensor(v, v, hc[:, k % 2], ALU.add).then_inc(y_added, 1)
            nc.gpsimd.tensor_copy(state[:, k, :], hs[:, k % 2, :, GR - 1]).then_inc(state_kept, 1)

        def tail_item(g, k):
            m = K * (g - 2) + k
            pool.wait_ge(scanned, H * (m + 1))
            pool.wait_ge(c_kept, m + 1 - K * (G - 2))
            pool.wait_ge(mm_done, K * G)
            pool.wait_ge(y_added, m - 1)
            nc.gpsimd.tensor_tensor(tail_hc[:, k % 2], hs[:, k % 2],
                                    tail_c[:, k % 2:k % 2 + 1, :].to_broadcast([P, H, GR]),
                                    ALU.mult).then_inc(hc_ready, 1)
            nc.gpsimd.tensor_copy(state[:, k, :], hs[:, k % 2, :, GR - 1]).then_inc(state_kept, 1)

        def body(g, par):
            for k in range(K):
                if isinstance(g, int) and (g, k) == (1, 0):
                    pool.wait_ge(done["h2_ready"], G)
                    nc.gpsimd.memset(state[:, :, :], 0.0).then_inc(zeros, 1)
                    nc.gpsimd.memset(xc[:, :, GR:], 0.0).then_inc(zeros, 1)
                    pool.wait_ge(zeros, 2)
                if k == 1 and prep_in(g):
                    after(pool, conv_done, H * (g - 1))
                    after(pool, dt_ready, g - 1)
                    last = xc[:, :, GR:GR + HIST]
                    nc.gpsimd.tensor_tensor(xc[:, :, 0:HIST], last, ones3, ALU.mult).then_inc(hist_ready, 1)
                if product_in(g):
                    pool.wait_ge(kept, JB * (K * g + k) + PARTED)
                    nc.gpsimd.tensor_tensor(lo[:, k % 2], full[:, :, :], hi[:, k % 2].bitcast(F32), ALU.subtract
                                            ).then_inc(lo_ready, 1)
                if k and items_in(g) and not tail(g):
                    add_item(g, par, k - 1)
                if k == 0 and items_in(g - 1) and not tail(g - 1):
                    add_item(g - 1, 1 - par, K - 1)
                if items_in(g) and tail(g):
                    tail_item(g, k)
                if k == 0 and final_in(g) and not tail(g - 1):
                    v = y[:, 1 - par]
                    pool.wait_ge(y_added, K * (g - 2))
                    pool.wait_ge(sz_ready, g - 2)
                    nc.gpsimd.tensor_tensor(v, v, sz[:, 1 - par], ALU.mult).then_inc(y_gated, 1)
                if k == 12 and prep_in(g):
                    pool.wait_ge(u_ready, g)
                    after(pool, out_ps, g - 2)
                    for h in range(H):
                        nc.gpsimd.tensor_tensor(y[:, 1 - par, h, :], u[:, h, :],
                                                d_sb[:, h:h + 1].to_broadcast([P, GR]), ALU.mult
                                                ).then_inc(y_start, 1)

        ones3 = one[:, 0:1].rearrange("p (a b) -> p a b", a=1).to_broadcast([P, H, HIST])
        pool.wait_ge(params, 16 * PARAMS)
        walk(body, pool)

    def scalar(act):
        act.wait_ge(params, 16 * PARAMS)
        nc.scalar.activation(a_sb[:, :, :], a_sb[:, :, :], ACT.Exp).then_inc(a_exp, 1)

        def exp_minus(v, src):
            nc.scalar.activation(v, src, ACT.Exp, scale=-1.0).then_inc(a_own, 1)

        def invert(step, n, g, ready):
            act.wait_ge(a_own, A_OWN * (g - 1) + n + step)
            if step == 0:
                nc.scalar.activation(sig[:, :, :], sig[:, :, :], ACT.Ln, bias=1.0).then_inc(a_own, 1)
            else:
                nc.scalar.activation(sig[:, :, :], sig[:, :, :], ACT.Exp, scale=-1.0).then_inc(ready, 1)

        def prep_first(g, par, k):
            if k == 1:
                act.wait_ge(mm_done, K * g)
                after(act, dt_ps, H * (g - 1))
                nc.scalar.activation(at[:, :], acc, ACT.Identity).then_inc(at_ready, 1)

        def prep_mid(g, par, k):
            if k == 9:
                invert(1, 2, g, sig_u)

        def prep_last(g, par, k):
            if k == 2:
                act.wait_ge(gcn_ps, g)
                after(act, bcs_ready, g - 1)
                nc.scalar.activation(hn[:, :, :], misc.rearrange("p (r d) -> p r d", r=RB), ACT.Relu
                                     ).then_inc(gcn_relu, 1)
            if k == 3:
                act.wait_ge(var_ready, g)
                nc.scalar.activation(root[:, :], var[:, :], ACT.Ln).then_inc(ln_ready, 1)
                act.wait_ge(ln_ready, g)
                nc.scalar.activation(root[:, :], root[:, :], ACT.Exp, scale=-0.5).then_inc(root_ready, 1)
            if k == 5:
                act.wait_ge(hn_turned, g)
                after(act, xz_ps, 4 * (g - 1))
                nc.scalar.activation(ht[:, :], misc, ACT.Identity, scale=ln_g_sb[:, 0:1], bias=ln_b_sb[:, 0:1]
                                     ).then_inc(ht_ready, 1)
            if k in (6, 7, 8, 9):
                q = k - 6
                act.wait_ge(xz_ps, 4 * (g - 1) + q + 1)
                if q == 0:
                    act.wait_ge(hist_ready, g)
                if q == 2:
                    after(act, dt_ready, g - 1)
                dst = xc[:, q, HIST:] if q < H else zr[:, q - H, :]
                nc.scalar.activation(dst, misc, ACT.Identity).then_inc(xz_ready, 1)
            if k in (7, 8):
                h = k - 7
                act.wait_ge(conv_done, H * (g - 1) + h + 1)
                after(act, dt_ready, g - 1)
                exp_minus(sig[:, h, :], conv[:, h, :])
            if k == 8:
                invert(0, 2, g, sig_u)
            if k == 10:
                act.wait_ge(u_ready, g)
                act.wait_ge(xz_ready, 4 * g)
                exp_minus(sig[:, :, :], zr[:, :, :])
            if k == 11:
                invert(0, 4, g, sig_z)
                invert(1, 4, g, sig_z)
            if k in (12, 13):
                h = k - 12
                act.wait_ge(dt_ps, H * (g - 1) + h + 1)
                nc.scalar.activation(conv[:, h, :], misc, ACT.Identity, bias=b_dt_sb[:, h:h + 1]
                                     ).then_inc(dt_arg, 1)
                act.wait_ge(dt_arg, H * (g - 1) + h + 1)
                act.wait_ge(sz_ready, g)
                nc.scalar.activation(sig[:, h, :], conv[:, h, :], ACT.Abs).then_inc(a_own, 1)
            if k == 13:
                act.wait_ge(a_own, A_OWN * (g - 1) + 7)
                exp_minus(sig[:, :, :], sig[:, :, :])
            if k == 14:
                act.wait_ge(a_own, A_OWN * g)
                nc.scalar.activation(zr[:, :, :], sig[:, :, :], ACT.Ln, bias=1.0).then_inc(soft_ready, 1)

        def rates(g, par, k):
            after(act, scanned, H * (K * (g - 2) + k - 1))
            if isinstance(g, int) and (g, k) == (2, 0):
                act.wait_ge(a_ready, 1)
            if k == 0:
                act.wait_ge(dt_ready, g - 1)
            for h in range(H):
                nc.scalar.activation(da[:, k % 2, h, :], dt[:, par, h, :], ACT.Exp,
                                     scale=a_sb[:, h, k:k + 1]).then_inc(da_ready, 1)

        def body(g, par):
            for k in range(K):
                if prep_in(g):
                    prep_first(g, par, k)
                if product_in(g):
                    if isinstance(g, int) and (g, k) == (0, 0):
                        act.wait_ge(done["mm_done"], K * G)
                    after(act, mm_done, K * g + k - 1)
                    after(act, lo_ready, K * g + k)
                for b in range(JB):
                    if product_in(g):
                        act.wait_ge(turned, JB * (K * g + k) + b + 1)
                        if b < PARTED:
                            nc.scalar.activation(full[:, b, :], bank(b % 2), ACT.Identity)
                        dst = hi[:, k % 2, b, :] if b < PARTED else whole[:, k % 2, b - PARTED, :]
                        nc.scalar.activation(dst, bank(b % 2), ACT.Identity).then_inc(kept, 1)
                    if b == 1 and prep_in(g):
                        prep_mid(g, par, k)
                    if b == 1 and items_in(g):
                        rates(g, par, k)
                    if b == 1 and items_in(g) and tail(g):
                        m = K * (g - 2) + k
                        act.wait_ge(bc_ps, m + 1)
                        act.wait_ge(lo_ready, K * G)
                        act.wait_ge(hc_ready, m - 1)
                        nc.scalar.activation(tail_c[:, k % 2, :], c_ps[k % 2], ACT.Identity).then_inc(c_kept, 1)
                if isinstance(g, int) and (g, k) == (0, 1):
                    last_steps["root"](act)
                if prep_in(g):
                    prep_last(g, par, k)

        walk(body, act)

    def vector(dve):
        chain = Chain(dve, v_own)
        dve.wait_ge(params, 16 * PARAMS)
        dve.wait_ge(a_exp, 1)
        nc.vector.tensor_scalar(a_sb[:, :, :], a_sb[:, :, :], -1.0, None, ALU.mult).then_inc(a_ready, 1)

        def prep(g, par, k, last):
            o = OWN * (g - 1)
            if (k, last) == (3, False):
                dve.wait_ge(gcn_relu, g)
                for r in range(RB):
                    ins = nc.vector.bn_stats(stats[:, r, :], hn[:, r, :])
                chain(ins, o + 1)
                *most, final_step = variance_steps(nc, stats, mean[:, :], var[:, :], work[:, :])
                for n, step in enumerate(most):
                    chain(step(), o + 2 + n)
                final_step().then_inc(var_ready, 1)
            if (k, last) == (4, False):
                dve.wait_ge(var_ready, g)
                dve.wait_ge(root_ready, g)
                for n, step in enumerate(newton_steps(nc, root[:, :], var[:, :], work[:, :])):
                    chain(step(), o + VARIANCE + 1 + n)
                for r in range(RB):
                    ins = nc.vector.tensor_scalar(hn[:, r, :], hn[:, r, :], mean[:, r:r + 1], root[:, r:r + 1],
                                                  ALU.subtract, ALU.mult)
                ins.then_inc(hn_ready, 1)
            o += NORM
            if k in (7, 8) and not last:
                h = k - 7
                dve.wait_ge(xz_ready, 4 * (g - 1) + h + 1)
                dve.wait_ge(hist_ready, g)
                after(dve, dt_ready, g - 1)
                nc_first = nc.vector.tensor_scalar(conv[:, h, :], xc[:, h, 0:GR], conv_w_sb[:, h, 0:1],
                                                   conv_b_sb[:, h:h + 1], ALU.mult, ALU.add)
                chain(nc_first, o + TAPS * h + 1)
                for t in range(1, TAPS):
                    ins = nc.vector.scalar_tensor_tensor(out=conv[:, h, :], in0=xc[:, h, t:t + GR],
                                                         scalar=conv_w_sb[:, h, t:t + 1], in1=conv[:, h, :],
                                                         op0=ALU.mult, op1=ALU.add)
                    if t < TAPS - 1:
                        chain(ins, o + TAPS * h + 1 + t)
                    else:
                        ins.then_inc(conv_done, 1)
                        dve.wait_ge(conv_done, H * (g - 1) + h + 1)
                        dve.sem_inc(v_own, 1)
            o += CONV
            if (k, last) == (9, True):
                dve.wait_ge(sig_u, g)
                after(dve, dtu_ready, g - 1)
                after(dve, y_start, H * (g - 1))
                nc.vector.tensor_tensor(u[:, :, :], conv[:, :, :], sig[:, :, :], ALU.mult).then_inc(u_ready, 1)
            if (k, last) == (12, False):
                dve.wait_ge(sig_z, g)
                after(dve, y_gated, g - 2)
                nc.vector.tensor_tensor(sz[:, 1 - par], zr[:, :, :], sig[:, :, :], ALU.mult).then_inc(sz_ready, 1)
            if (k, last) == (11, False):
                full, parts = misc[0:3 * BC, :], bcs[:, 1 - par, :]
                dve.wait_ge(xp_ps, g)
                after(dve, bc_ps, K * (g - 2))
                nc.vector.tensor_copy(dtr[3 * BC:3 * BC + RANK, :], misc[3 * BC:3 * BC + RANK, :]
                                      ).then_inc(xp_read, 1)
                chain(nc.vector.tensor_copy(parts, full), o + 1)
                nc.vector.tensor_tensor(rest[0:3 * BC, :], full, parts, ALU.subtract).then_inc(xp_read, 1)
                dve.wait_ge(xp_read, 2 * g)
                chain(nc.vector.tensor_copy(parts[BC:2 * BC, :], rest[BC:2 * BC, :]), o + 2)
                chain(nc.vector.tensor_copy(parts[2 * BC:, :], rest[2 * BC:3 * BC, :]), o + 3)
                chain(nc.vector.tensor_tensor(rest[2 * BC:3 * BC, :], rest[2 * BC:3 * BC, :], parts[2 * BC:, :],
                                              ALU.subtract), o + 4)
                chain(nc.vector.tensor_copy(parts[2 * BC:, :], rest[2 * BC:3 * BC, :]), o + 5)
                dve.sem_inc(bcs_ready, 1)
            o += PARTS
            if (k, last) == (15, False):
                dve.wait_ge(soft_ready, g)
                chain(nc.vector.tensor_scalar(low[:, :, :], sig[:, :, :], 1.0, 1.0, ALU.add, ALU.subtract), o + 1)
                chain(nc.vector.tensor_tensor(low[:, :, :], sig[:, :, :], low[:, :, :], ALU.subtract), o + 2)
                chain(nc.vector.tensor_tensor(low[:, :, :], low[:, :, :], zr[:, :, :], ALU.add), o + 3)
                after(dve, da_ready, H * K * (g - 2))
                nc.vector.scalar_tensor_tensor(out=dt[:, 1 - par], in0=conv[:, :, :], scalar=0.0,
                                               in1=low[:, :, :], op0=ALU.max, op1=ALU.add).then_inc(dt_ready, 1)
            if (k, last) == (15, True):
                dve.wait_ge(dt_ready, g)
                after(dve, dbu_ready, K * (g - 2))
                nc.vector.tensor_tensor(dtu[:, 1 - par], dt[:, 1 - par], u[:, :, :], ALU.mult
                                        ).then_inc(dtu_ready, 1)

        def item(g, par, k):
            m = K * (g - 2) + k
            b = k % 2
            dve.wait_ge(bc_ps, m + 1)
            dve.wait_ge(dtu_ready, g - 1)
            if not tail(g) or (g == G and k < 2):
                after(dve, y_added, m - 1)
            nc.vector.tensor_tensor(dbu[:, b], dtu[:, par],
                                    b_ps[b].rearrange("p (o t) -> p o t", o=1).to_broadcast([P, H, GR]), ALU.mult
                                    ).then_inc(dbu_ready, 1)
            dve.wait_ge(dbu_ready, m + 1)
            dve.wait_ge(da_ready, H * (m + 1))
            after(dve, state_kept, m - 1)
            after(dve, hc_ready, m - 1)
            for h in range(H):
                nc.vector.tensor_tensor_scan(hs[:, b, h, :], da[:, b, h, :], dbu[:, b, h, :],
                                             state[:, k, h:h + 1], ALU.mult, ALU.add).then_inc(scanned, 1)
            if tail(g):
                return
            dve.wait_ge(scanned, H * (m + 1))
            nc.vector.tensor_tensor(hc[:, b], hs[:, b],
                                    c_ps[b].rearrange("p (o t) -> p o t", o=1).to_broadcast([P, H, GR]), ALU.mult
                                    ).then_inc(hc_ready, 1)

        def body(g, par):
            for k in range(K):
                if k == 0 and final_in(g) and tail(g - 1):
                    v = y[:, 1 - par]
                    dve.wait_ge(y_added, K * (g - 2))
                    dve.wait_ge(y_start, H * (g - 2))
                    nc.vector.tensor_tensor(v, v, y_sum, ALU.add).then_inc(y_summed, 1)
                    dve.wait_ge(y_summed, g - G)
                    nc.vector.tensor_tensor(v, v, sz[:, 1 - par], ALU.mult).then_inc(y_gated, 1)
                if k == FINAL_AT + 1 and final_in(g):
                    dve.wait_ge(out_ps, g - 2)
                    dve.wait_ge(x1g_here, 16 * (g - 2))
                    nc.vector.tensor_tensor(og[:, :, :], misc.rearrange("p (r d) -> p r d", r=RB), og[:, :, :],
                                            ALU.add).then_inc(og_ready, 1)
                if prep_in(g):
                    prep(g, par, k, False)
                if items_in(g):
                    item(g, par, k)
                if prep_in(g):
                    prep(g, par, k, True)

        walk(body, dve)

    def tensor(pe):
        pe.wait_ge(params, 16 * PARAMS)
        pe.wait_ge(consts, 6)

        def turn(g, k, b):
            n = JB * (K * g + k) + b
            if b == 0:
                pe.wait_ge(adj_here[k % SLOTS], 16 * (K // SLOTS * g + k // SLOTS + 1))
            after(pe, kept, n - 1)
            for r in range(RB):
                ins = nc.tensor.transpose(bank(b % 2)[:, r * P:(r + 1) * P],
                                          adj_slot[:, k % SLOTS, r, b * P:(b + 1) * P], ident[:, :])
            ins.then_inc(turned, 1)

        def multiply(g, k, b):
            j = k * JB + b
            first, last = j == PARTED, j == N // P - JB + PARTED - 1
            if isinstance(g, int) and g == 0:
                pe.wait_ge(done["h2_ready"], k + 1)
            if first:
                after(pe, at_ready, g)
            if b < PARTED:
                pe.wait_ge(lo_ready, K * g + k + 1)
                h_hi, h_lo = h2_hi[:, k * PARTED + b, :], h2_lo[:, k * PARTED + b, :]
                a_hi, a_lo = hi[:, k % 2, b, :], lo[:, k % 2, b, :]
                nc.tensor.matmul(acc, h_hi, a_hi, start=False, stop=False)
                nc.tensor.matmul(acc, h_lo, a_hi, start=False, stop=False)
                ins = nc.tensor.matmul(acc, h_hi, a_lo, start=False, stop=last)
            else:
                pe.wait_ge(kept, JB * (K * g + k) + b + 1)
                h = h2[:, k * (JB - PARTED) + b - PARTED, :]
                ins = nc.tensor.matmul(acc, h, whole[:, k % 2, b - PARTED, :], start=first, stop=False)
            if b == PARTED - 1:
                ins.then_inc(mm_done, 1)

        def prep(g, par, k):
            if k == 2:
                pe.wait_ge(at_ready, g)
                after(pe, dt_arg, H * (g - 1))
                for r in range(RB):
                    part = misc[:, r * D:(r + 1) * D]
                    nc.tensor.matmul(part, ones_row[:, :], gcn_b_row[:, :], start=True, stop=False)
                    ins = nc.tensor.matmul(part, at[:, r * P:(r + 1) * P], gcn_w_sb[:, :],
                                           start=False, stop=True)
                ins.then_inc(gcn_ps, 1)
            if k == 5:
                pe.wait_ge(hn_ready, g)
                pe.wait_ge(gcn_relu, g)
                if final_in(g):
                    pe.wait_ge(og_ready, g - 2)
                for r in range(RB):
                    ins = nc.tensor.transpose(misc[:, r * P:(r + 1) * P], hn[:, r, :], ident[:, :])
                ins.then_inc(hn_turned, 1)
            if k in (6, 7, 8, 9):
                q = k - 6
                pe.wait_ge(ht_ready, g)
                if q:
                    pe.wait_ge(xz_ready, 4 * (g - 1) + q)
                nc.tensor.matmul(misc, w_in_sb[:, q * P:(q + 1) * P], ht[:, :], start=True, stop=True
                                 ).then_inc(xz_ps, 1)
            if k == 10:
                pe.wait_ge(u_ready, g)
                pe.wait_ge(xz_ready, 4 * g)
                for h in range(H):
                    ins = nc.tensor.matmul(misc[0:3 * BC + RANK, :], w_xp_sb[:, h, :], u[:, h, :],
                                           start=(h == 0), stop=(h == H - 1))
                ins.then_inc(xp_ps, 1)
            if k in (12, 13):
                h = k - 12
                pe.wait_ge(xp_read, 2 * g)
                if h:
                    pe.wait_ge(dt_arg, H * (g - 1) + h)
                nc.tensor.matmul(misc, w_dt_sb[3 * BC:3 * BC + RANK, h * P:(h + 1) * P],
                                 dtr[3 * BC:3 * BC + RANK, :], start=True, stop=True).then_inc(dt_ps, 1)

        def spread(g, par, k):
            m = K * (g - 2) + k
            if k == 0:
                pe.wait_ge(bcs_ready, g - 1)
            if tail(g) and (g > G or k >= 2):
                pe.wait_ge(dbu_ready, m - 1)
                pe.wait_ge(c_kept, m - 1 - K * (G - 2))
            else:
                after(pe, hc_ready, m - 1)
            nc.tensor.matmul(b_ps[k % 2], pick[:, k, :], bcs[:, par, :], start=True, stop=True)
            nc.tensor.matmul(c_ps[k % 2], pick[:, S + k, :], bcs[:, par, :], start=True, stop=True
                             ).then_inc(bc_ps, 1)

        def add_item(g, k):
            m = K * (g - 2) + k
            pe.wait_ge(hc_ready, m + 1)
            if k == 0 and g > G:
                pe.wait_ge(y_summed, g - G)
            for h in range(H):
                ins = nc.tensor.matmul(y_sum[:, h, :], ident[:, :], tail_hc[:, k % 2, h, :],
                                       start=(k == 0), stop=(k == K - 1))
            ins.then_inc(y_added, 1)

        def final(g, par):
            v = y[:, 1 - par]
            pe.wait_ge(y_gated, g - 2)
            if prep_in(g):
                pe.wait_ge(gcn_relu, g)
            else:
                pe.wait_ge(dt_arg, H * G)
                after(pe, og_ready, g - 3)
            for r in range(RB):
                for h in range(H):
                    ins = nc.tensor.matmul(misc[:, r * D:(r + 1) * D], v[:, h, r * P:(r + 1) * P],
                                           w_out_sb[:, h, :], start=(h == 0), stop=(h == H - 1))
            ins.then_inc(out_ps, 1)

        def body(g, par):
            if final_in(g) and tail(g - 1):
                for k in range(K - 2, K):
                    add_item(g - 1, k)
            for k in range(K):
                for b in range(JB):
                    if product_in(g):
                        turn(g, k, b)
                    if isinstance(g, int) and (g, k, b) == (0, 0, 1):
                        last_steps["turn"](pe)
                    if b % 2:
                        for q in ((b + 1) % JB, (b + 2) % JB):
                            if k and product_in(g):
                                multiply(g, k - 1, q)
                            if k == 0 and prep_in(g):
                                multiply(g - 1, K - 1, q)
                    if b == 1 and items_in(g):
                        spread(g, par, k)
                    if b == 1 and k >= 2 and items_in(g) and tail(g):
                        add_item(g, k - 2)
                    if b == 1 and prep_in(g):
                        prep(g, par, k)
                    if b == 1 and k == FINAL_AT and final_in(g):
                        final(g, par)

        walk(body, pe)

    return sync, gpsimd, scalar, vector, tensor


def build(nc, x, adj, L0_gnn_W, L0_gnn_B, L1_gnn_gcn_w, L1_gnn_gcn_b, L1_gnn_ln_g, L1_gnn_ln_b, L1_gnn_w_in,
          L1_gnn_conv_w, L1_gnn_conv_b, L1_gnn_w_xp, L1_gnn_w_dt, L1_gnn_b_dt, L1_gnn_A_log, L1_gnn_D_skip,
          L1_gnn_w_out, out):
    with ExitStack() as both:
        def sem(name):
            return both.enter_context(nc.semaphore(name))

        def shared(name, shape, dt=F32):
            return both.enter_context(nc.sbuf_tensor(name, shape, dt))

        h2 = shared("h2", [P, (JB - PARTED) * G, D])
        h2_hi = shared("h2_hi", [P, PARTED * G, D], F32R)
        h2_lo = shared("h2_lo", [P, PARTED * G, D], F32R)
        adj_slot = shared("adj_slot", [P, SLOTS, RB, CW])
        ident = shared("ident", [P, P])
        p = parameters(nc, both, sem, L1_gnn_gcn_w, L1_gnn_gcn_b, L1_gnn_ln_g, L1_gnn_ln_b, L1_gnn_w_in,
                       L1_gnn_conv_w, L1_gnn_conv_b, L1_gnn_w_xp, L1_gnn_w_dt, L1_gnn_b_dt, L1_gnn_A_log,
                       L1_gnn_D_skip, L1_gnn_w_out)
        done = {name: sem(name) for name in ("turned", "mm_done", "x1_ready", "x1_kept", "h2_ready")}
        with ExitStack() as ctx:
            programs, last_steps = layer1(nc, ctx, sem, x, adj, L0_gnn_W, L0_gnn_B, out, h2, h2_hi, h2_lo,
                                          adj_slot, ident, p, done)
            sync1, gpsimd1, scalar1, vector1, tensor1 = programs
        with ExitStack() as ctx:
            sync2, gpsimd2, scalar2, vector2, tensor2 = layer2(
                nc, ctx, sem, adj, p, out, h2, h2_hi, h2_lo, adj_slot, ident, done, last_steps)
            with nc.Block() as block:
                @block.sync
                def _(sp):
                    sync1(sp)
                    sync2(sp)

                @block.gpsimd
                def _(pool):
                    gpsimd1(pool)
                    gpsimd2(pool)

                @block.scalar
                def _(act):
                    scalar1(act)
                    scalar2(act)

                @block.vector
                def _(dve):
                    vector1(dve)
                    vector2(dve)

                @block.tensor
                def _(pe):
                    tensor1(pe)
                    tensor2(pe)


_INS = ['x', 'adj', 'L0_gnn_W', 'L0_gnn_B', 'L1_gnn_gcn_w', 'L1_gnn_gcn_b', 'L1_gnn_ln_g', 'L1_gnn_ln_b',
        'L1_gnn_w_in', 'L1_gnn_conv_w', 'L1_gnn_conv_b', 'L1_gnn_w_xp', 'L1_gnn_w_dt', 'L1_gnn_b_dt',
        'L1_gnn_A_log', 'L1_gnn_D_skip', 'L1_gnn_w_out']


def kernel(**inputs):
    import numpy as _np
    import concourse.bacc as _bacc
    from concourse import mybir as _mybir
    from concourse.bass_utils import run_bass_kernel_spmd as _run

    nc = _bacc.Bacc("TRN2", target_bir_lowering=False, num_devices=1)
    arrays, args = {}, []
    for name in _INS:
        a = _np.ascontiguousarray(inputs[name])
        arrays[f"in_{name}_dram"] = a
        args.append(nc.dram_tensor(f"in_{name}_dram", a.shape, _mybir.dt.from_np(a.dtype), kind="ExternalInput").ap())
    out = nc.dram_tensor("out_0_dram", (N, D), _mybir.dt.float32, kind="ExternalOutput").ap()
    build(nc, *args, out)
    r = _run(nc, [arrays], core_ids=[0])
    return r.results[0]["out_0_dram"]
```
